# Optimizing a Trainium2 kernel written in Bass

```python
import numpy as np
import jax
import jax.numpy as jnp

def _softmax(x, axis=-1):
    return jax.nn.softmax(x, axis=axis)
def _gelu(x):
    return jax.nn.gelu(x, approximate=True)
def _silu(x):
    return jax.nn.silu(x)
def _sigmoid(x):
    return jax.nn.sigmoid(x)
def _layernorm(x, axis=-1, eps=1e-5):
    m = jnp.mean(x, axis=axis, keepdims=True)
    v = jnp.var(x, axis=axis, keepdims=True)
    return (x - m) / jnp.sqrt(v + eps)
def _scatter_add(tgt, idx, src, axis=0):
    return tgt.at[idx].add(src)
def _segment_sum(src, seg, n):
    return jax.ops.segment_sum(src, seg, n)

kernel_name = 'mk_conv_preact_d2_conv_nhwc768_c8d5a5'

def setup_inputs(seed: int = 0):
    np.random.seed(seed)
    _w = jnp.asarray
    def _rec_inputs():
        import jax
        import jax.numpy as jnp
        _gk = jax.random.key(seed)
        x = -0.0005963 + 1.001 * jax.random.normal(jax.random.fold_in(_gk, 1), (4, 32, 32, 768), jnp.float32)
        return x
    x = _rec_inputs()
    def _L0_conv_setup():
        import jax, jax.numpy as jnp
        import numpy as np
        B, H, W, C = (4, 32, 32, 768)
        NH = 12
        HD = C // NH

        def _get_rel_pos(q_size, k_size, rel_pos):
            q_coords = jnp.arange(q_size)[:, None] * max(k_size / q_size, 1.0)
            k_coords = jnp.arange(k_size)[None, :] * max(q_size / k_size, 1.0)
            rel = (q_coords - k_coords + (k_size - 1) * max(q_size / k_size, 1.0)).astype(jnp.int32)
            return rel_pos[rel]
        key = jax.random.key(seed)
        ks = jax.random.split(key, 12)
        s = 1.0 / np.sqrt(C)
        return {'hidden_states': jax.random.normal(ks[0], (B, H, W, C), jnp.float32), 'Wq': jax.random.normal(ks[1], (C, C), jnp.float32) * s, 'bq': jax.random.normal(ks[2], (C,), jnp.float32) * 0.02, 'Wk': jax.random.normal(ks[3], (C, C), jnp.float32) * s, 'bk': jax.random.normal(ks[4], (C,), jnp.float32) * 0.02, 'Wv': jax.random.normal(ks[5], (C, C), jnp.float32) * s, 'bv': jax.random.normal(ks[6], (C,), jnp.float32) * 0.02, 'Wp': jax.random.normal(ks[7], (C, C), jnp.float32) * s, 'bp': jax.random.normal(ks[8], (C,), jnp.float32) * 0.02, 'rel_h': jax.random.normal(ks[9], (2 * H - 1, HD), jnp.float32) * 0.02, 'rel_w': jax.random.normal(ks[10], (2 * W - 1, HD), jnp.float32) * 0.02}
    _L0_conv_all = _L0_conv_setup()
    _L0_conv_in = {k: v for k, v in _L0_conv_all.items() if k in ('Wq', 'bq', 'Wk', 'bk', 'Wv', 'bv', 'Wp', 'bp', 'rel_h', 'rel_w', )}
    del _L0_conv_all

    def _L1_conv_setup():
        import jax, jax.numpy as jnp
        import numpy as np
        D_MODEL = 768
        D_HEAD = 64
        N_HEADS = D_MODEL // D_HEAD
        KERNEL = 7
        H = 64
        W = 64
        BATCH = 1

        def _neighbour_indices(h, w, k):
            r = k // 2
            ci = jnp.clip(jnp.arange(h), r, w - 1 - r)
            cj = jnp.clip(jnp.arange(w), r, h - 1 - r)
            off = jnp.arange(k) - r
            rows = ci[:, None] + off
            cols = cj[:, None] + off
            flat = rows[:, None, :, None] * w + cols[None, :, None, :]
            return flat.reshape(h * w, k * k)
        key = jax.random.key(seed)
        k1, k2, k3 = jax.random.split(key, 3)
        x = jax.random.normal(k1, (BATCH, H, W, D_MODEL), dtype=jnp.float32)
        qkv_w = jax.random.normal(k2, (3 * D_MODEL, D_MODEL), dtype=jnp.float32) * 0.02
        out_w = jax.random.normal(k3, (D_MODEL, D_MODEL), dtype=jnp.float32) * 0.02
        return {'x': x, 'qkv_w': qkv_w, 'out_w': out_w}
    _L1_conv_all = _L1_conv_setup()
    _L1_conv_in = {k: v for k, v in _L1_conv_all.items() if k in ('qkv_w', 'out_w', )}
    del _L1_conv_all

    return {
        "x": x,
        "L0_conv_Wq": _L0_conv_in["Wq"],
        "L0_conv_bq": _L0_conv_in["bq"],
        "L0_conv_Wk": _L0_conv_in["Wk"],
        "L0_conv_bk": _L0_conv_in["bk"],
        "L0_conv_Wv": _L0_conv_in["Wv"],
        "L0_conv_bv": _L0_conv_in["bv"],
        "L0_conv_Wp": _L0_conv_in["Wp"],
        "L0_conv_bp": _L0_conv_in["bp"],
        "L0_conv_rel_h": _L0_conv_in["rel_h"],
        "L0_conv_rel_w": _L0_conv_in["rel_w"],
        "L1_conv_qkv_w": _L1_conv_in["qkv_w"],
        "L1_conv_out_w": _L1_conv_in["out_w"],
    }

def reference(x, L0_conv_Wq, L0_conv_bq, L0_conv_Wk, L0_conv_bk, L0_conv_Wv, L0_conv_bv, L0_conv_Wp, L0_conv_bp, L0_conv_rel_h, L0_conv_rel_w, L1_conv_qkv_w, L1_conv_out_w):
    import jax
    import jax.numpy as jnp
    def _L0_conv_ref(hidden_states, Wq, bq, Wk, bk, Wv, bv, Wp, bp, rel_h, rel_w):
        import jax, jax.numpy as jnp
        import numpy as np
        B, H, W, C = (4, 32, 32, 768)
        NH = 12
        HD = C // NH

        def _get_rel_pos(q_size, k_size, rel_pos):
            q_coords = jnp.arange(q_size)[:, None] * max(k_size / q_size, 1.0)
            k_coords = jnp.arange(k_size)[None, :] * max(q_size / k_size, 1.0)
            rel = (q_coords - k_coords + (k_size - 1) * max(q_size / k_size, 1.0)).astype(jnp.int32)
            return rel_pos[rel]
        b, h, w, c = hidden_states.shape
        hw = h * w
        x = hidden_states.reshape(b, hw, c)

        def heads(t):
            return t.reshape(b, hw, NH, HD).transpose(0, 2, 1, 3).reshape(b * NH, hw, HD)
        q = heads(x @ Wq + bq)
        k = heads(x @ Wk + bk)
        v = heads(x @ Wv + bv)
        attn = jnp.einsum('bqd,bkd->bqk', q, k) / np.sqrt(HD)
        Rh = _get_rel_pos(h, h, rel_h)
        Rw = _get_rel_pos(w, w, rel_w)
        rq = q.reshape(b * NH, h, w, HD)
        rel_bias_h = jnp.einsum('bhwc,hkc->bhwk', rq, Rh)
        rel_bias_w = jnp.einsum('bhwc,wkc->bhwk', rq, Rw)
        attn = (attn.reshape(b * NH, h, w, h, w) + rel_bias_h[:, :, :, :, None] + rel_bias_w[:, :, :, None, :]).reshape(b * NH, hw, hw)
        attn = jax.nn.softmax(attn, axis=-1)
        out = jnp.einsum('bqk,bkd->bqd', attn, v)
        out = out.reshape(b, NH, h, w, HD).transpose(0, 2, 3, 1, 4).reshape(b, h, w, c)
        return out @ Wp + bp

    def _L1_conv_ref(x, qkv_w, out_w):
        import jax, jax.numpy as jnp
        import numpy as np
        D_MODEL = 768
        D_HEAD = 64
        N_HEADS = D_MODEL // D_HEAD
        KERNEL = 7
        H = 64
        W = 64
        BATCH = 1

        def _neighbour_indices(h, w, k):
            r = k // 2
            ci = jnp.clip(jnp.arange(h), r, w - 1 - r)
            cj = jnp.clip(jnp.arange(w), r, h - 1 - r)
            off = jnp.arange(k) - r
            rows = ci[:, None] + off
            cols = cj[:, None] + off
            flat = rows[:, None, :, None] * w + cols[None, :, None, :]
            return flat.reshape(h * w, k * k)
        n, h, w, d = x.shape
        s = h * w
        k2 = KERNEL * KERNEL
        idx = _neighbour_indices(h, w, KERNEL)
        qkv = jnp.einsum('nsd,fd->nsf', x.reshape(n, s, d), qkv_w)
        qkv = qkv.reshape(n, s, 3, N_HEADS, D_HEAD)
        q = jnp.transpose(qkv[:, :, 0], (0, 2, 1, 3))
        kk = jnp.transpose(qkv[:, :, 1], (0, 2, 1, 3))
        v = jnp.transpose(qkv[:, :, 2], (0, 2, 1, 3))
        kg = kk[:, :, idx, :]
        vg = v[:, :, idx, :]
        scale = 1.0 / jnp.sqrt(jnp.asarray(D_HEAD, dtype=q.dtype))
        scores = jnp.einsum('bnse,bnske->bnsk', q, kg) * scale
        attn = jax.nn.softmax(scores, axis=-1)
        o = jnp.einsum('bnsk,bnske->bnse', attn, vg)
        o = jnp.transpose(o, (0, 2, 1, 3)).reshape(n, s, N_HEADS * D_HEAD)
        out = jnp.einsum('nsd,fd->nsf', o, out_w)
        return out.reshape(n, h, w, d)

    def _gn(v, G=32, eps=1e-5):
        B_, H_, W_, C_ = v.shape
        g = v.reshape(B_, H_, W_, G, C_ // G)
        m = jnp.mean(g, axis=(1, 2, 4), keepdims=True)
        s = jnp.var(g, axis=(1, 2, 4), keepdims=True)
        return ((g - m) / jnp.sqrt(s + eps)).reshape(v.shape)

    def _ln_c(v, eps=1e-6):
        m = jnp.mean(v, axis=-1, keepdims=True)
        s = jnp.var(v, axis=-1, keepdims=True)
        return (v - m) / jnp.sqrt(s + eps)

    def _ln_t(v, eps=1e-5):
        m = jnp.mean(v, axis=-1, keepdims=True)
        s = jnp.var(v, axis=-1, keepdims=True)
        return (v - m) / jnp.sqrt(s + eps)

    def _to_tokens(v):
        B_, H_, W_, C_ = v.shape
        return v.reshape(B_, H_ * W_, C_)
    def _from_tokens(t, like):
        return t.reshape(like.shape)

    x = x + _L0_conv_ref(_gn(x), L0_conv_Wq, L0_conv_bq, L0_conv_Wk, L0_conv_bk, L0_conv_Wv, L0_conv_bv, L0_conv_Wp, L0_conv_bp, L0_conv_rel_h, L0_conv_rel_w)
    x = x + _L1_conv_ref(_gn(x), L1_conv_qkv_w, L1_conv_out_w)
    return x


_drawn_inputs = setup_inputs


def setup_inputs(seed=0):
    import zlib

    import numpy as np

    out = dict(_drawn_inputs(seed))
    spreads = {}
    factors = {'L0_conv_bq': 8.0,
     'L0_conv_bk': 8.0,
     'L0_conv_bp': 2.787,
     'L0_conv_rel_h': 6.712,
     'L0_conv_rel_w': 6.785}
    for name, (base, spread) in spreads.items():
        noise = np.random.default_rng([zlib.crc32(name.encode()), seed]).standard_normal(out[name].shape)
        drawn = base * np.exp(spread * noise) if base else spread * noise
        out[name] = jnp.asarray(drawn.astype(out[name].dtype))
    for name, factor in factors.items():
        out[name] = (out[name] * factor).astype(out[name].dtype)
    return out
```

```python
import concourse.bass as bass
from concourse import mybir

F32 = mybir.dt.float32
F32R = mybir.dt.float32r
ALU = mybir.AluOpType
ACT = mybir.ActivationFunctionType
AX = mybir.AxisListType

IMAGES, SIDE, CHANNELS, HEADS, LAYERS = 4, 32, 768, 12, 2
TOKENS = SIDE * SIDE
HEAD_DIM = CHANNELS // HEADS
CT = CHANNELS // 128
QT = TOKENS // 128
HALF = TOKENS // 2
CHUNK = 256
QK_CHUNKS, V_CHUNKS, O_CHUNKS = 6, 3, 3
CHUNKS = QK_CHUNKS + V_CHUNKS + O_CHUNKS
QK_TILES = 2 * CT
REL = 2 * SIDE - 1
GROUP = CHANNELS // 32
GROUP_SPAN = 3
EPS = 1e-5
REACH, RADIUS = 7, 3
P_SLOTS = 4
ORDER = [[0, 1, 2, 3, 4, 5, 6, 7], [0, 7, 1, 6, 2, 5, 3, 4]]


def centre(i):
    return min(max(i, RADIUS), SIDE - 1 - RADIUS)


def query_span(layer, key_tile):
    if layer == 0:
        return 0, TOKENS
    rows = range(4 * key_tile, 4 * key_tile + 4)
    near = [i for i in range(SIDE) if any(abs(centre(i) - r) <= RADIUS for r in rows)]
    return near[0] * SIDE, (near[-1] + 1) * SIDE


def key_span(query_tile):
    c = [centre(i) for i in range(4 * query_tile, 4 * query_tile + 4)]
    return (min(c) - RADIUS) * SIDE, (max(c) + RADIUS + 1) * SIDE


def group_blocks():
    return [(i, j) for j in range(GROUP_SPAN) for i in range(GROUP_SPAN) if abs(i - j) <= 1]


class Memory:

    def __init__(self, nc, at):
        self.nc, self.at = nc, at

    def put(self, name, shape, dtype=F32):
        size = 4
        for n in shape[1:]:
            size *= n
        t = self.nc.alloc_sbuf_tensor_at(name, shape, dtype, offset=self.at)
        self.at += (size + 31) // 32 * 32
        return t


def build(nc, x_in, w_in, bqk_in, scale_in, bv_in, bp_in, rel_in, onehot_in, mask_in, group_in,
          ident_in, y_out):
    blocks = group_blocks()
    m = Memory(nc, (nc.sbuf_base + 31) // 32 * 32)
    x = m.put("x", [128, CT, TOKENS])
    qk = m.put("qk", [128, QK_TILES, TOKENS])
    v = m.put("v", [128, QT, CHANNELS])
    k_hi = [m.put(f"k_hi{s}", [128, TOKENS], F32R) for s in range(2)]
    k_lo = [m.put(f"k_lo{s}", [128, TOKENS], F32R) for s in range(2)]
    q_max = [m.put(f"q_max{s}", [128, TOKENS], F32R) for s in range(2)]
    w_hi0 = m.put("w_hi0", [128, CT, CHUNK], F32R)
    w_lo0 = m.put("w_lo0", [128, CT, CHUNK], F32R)
    group = m.put("group", [128, len(blocks), 128])
    ident = m.put("ident", [128, 128], F32R)
    ones = m.put("ones", [128, 64])
    rel = m.put("rel", [128, 2, REL])
    bqk = m.put("bqk", [128, QK_TILES])
    scale = m.put("scale", [128, QK_TILES])
    bv = m.put("bv", [128, CT])
    bp = m.put("bp", [128, CT])
    bn = m.put("bn", [128, CT, 2, 6])
    mean_var = m.put("mean_var", [128, CT, 2])
    group_mv = m.put("group_mv", [128, CT, 2])
    shift2 = m.put("shift2", [128, 2, CT])
    variance = m.put("variance", [128, CT])
    power = m.put("power", [128, CT])
    rstd = m.put("rstd", [128, CT])
    max_part = m.put("max_part", [128, QT, 2])
    shared = m.at
    q_hi = [m.put(f"q_hi{s}", [128, TOKENS], F32R) for s in range(2)]
    q_lo = [m.put(f"q_lo{s}", [128, TOKENS], F32R) for s in range(2)]
    end = m.at
    m.at = shared
    w_hi1 = m.put("w_hi1", [128, CT, CHUNK], F32R)
    w_lo1 = m.put("w_lo1", [128, CT, CHUNK], F32R)
    raw = m.put("raw", [128, CT, CHUNK])
    m.at = max(m.at, end)
    w_hi, w_lo = [w_hi0, w_hi1], [w_lo0, w_lo1]
    shared = m.at
    a_hi = m.put("a_hi", [128, CT, TOKENS], F32R)
    a_lo = m.put("a_lo", [128, CT, TOKENS], F32R)
    assert m.at <= nc.sbuf_usable_end
    m.at = shared
    prob = m.put("prob", [128, P_SLOTS, TOKENS])
    acc = [m.put(f"acc{s}", [128, TOKENS]) for s in range(2)]
    v_head = [m.put(f"v_head{s}", [128, QT, HEAD_DIM]) for s in range(2)]
    q_rel = m.put("q_rel", [128, TOKENS])
    max_cols = m.put("max_cols", [128, 64 + QT * 128], F32R)
    recip = m.put("recip", [128, HALF])
    stage = m.put("stage", [128, TOKENS])

    score = nc.alloc_psum_tensor("score", [128, 2, 2, HALF], F32)
    small = nc.alloc_psum_tensor("small", [128, 2, HALF], F32)
    head_out = nc.alloc_psum_tensor("head_out", [128, 2, HALF], F32)
    small_all = small[:, :, :].rearrange("p a b -> p (a b)")

    def sem(name):
        return nc.alloc_semaphore(name)

    const_in, const_ok, stage_in = sem("const_in"), sem("const_ok"), sem("stage_in")
    x_in_sem, raw_in, y_sent = sem("x_in"), sem("raw_in"), sem("y_sent")
    bn_ok, mv_ok, gsum_ok, gmv_ok, shift_ok, shift2_ok = (sem(n) for n in (
        "bn_ok", "mv_ok", "gsum_ok", "gmv_ok", "shift_ok", "shift2_ok"))
    gshift_ok, var_ok, rstd_ok, normed = (sem(n) for n in ("gshift_ok", "var_ok", "rstd_ok", "normed"))
    a_hi_ok, a_lo_ok, w_hi_ok, w_lo_ok = (sem(n) for n in ("a_hi_ok", "a_lo_ok", "w_hi_ok", "w_lo_ok"))
    qk_mm, qk_ok, v_mm, v_ok, o_mm, o_ok = (sem(n) for n in (
        "qk_mm", "qk_ok", "v_mm", "v_ok", "o_mm", "o_ok"))
    mask_ok, cols_zero, o_hi_ok, o_lo_ok = (sem(n) for n in ("mask_ok", "cols_zero", "o_hi_ok", "o_lo_ok"))
    q_rel_ok, v_head_ok, q_hi_ok, k_hi_ok, q_max_ok, q_lo_ok, k_lo_ok = (sem(n) for n in (
        "q_rel_ok", "v_head_ok", "q_hi_ok", "k_hi_ok", "q_max_ok", "q_lo_ok", "k_lo_ok"))
    pos_mm, pos_hi_ok, pos_lo_ok = sem("pos_mm"), sem("pos_hi_ok"), sem("pos_lo_ok")
    max_mm, max_part_ok, max_cols_ok, max_row_mm, max_row_ok = (sem(n) for n in (
        "max_mm", "max_part_ok", "max_cols_ok", "max_row_mm", "max_row_ok"))
    score_ok, prob_ok, pv_done, added, sum_mm, recip_ok, head_done = (sem(n) for n in (
        "score_ok", "prob_ok", "pv_done", "added", "sum_mm", "recip_ok", "head_done"))
    acc_zero, recip_used = sem("acc_zero"), sem("recip_used")
    passed = {e.engine: sem(f"passed_{n}") for n, e in (
        ("tensor", nc.tensor), ("vector", nc.vector), ("gpsimd", nc.gpsimd), ("sync", nc.sync))}

    START = {id(prob_ok): 2, id(pv_done): P_SLOTS, id(added): P_SLOTS, id(head_done): 2,
             id(sum_mm): 2, id(qk_ok): 4, id(o_mm): 5, id(w_hi_ok): 1, id(w_lo_ok): 1}

    def start(s):
        return START.get(id(s), 0)

    def head_rows(s):
        return slice(64 * s, 64 * s + 64)

    def pos_rows(s):
        return slice(64 - 64 * s, 128 - 64 * s)

    def max_row(s):
        return 64 - 64 * s

    class At:

        def __init__(self, image, layer, pair=None, slot=None):
            self.image, self.layer, self.pair, self.slot = image, layer, pair, slot

        def phases(self, per, extra):
            return self.image * (2 * per) + (self.layer * per + extra)

        def layer0(self, per, extra):
            return self.image * per + extra

        def heads(self, per, extra):
            return self.image * (2 * HEADS * per) + self.pair * (2 * per) + (
                (self.layer * HEADS + self.slot) * per + extra)

        def heads2(self, per0, per1, extra):
            per = per1 if self.layer else per0
            return self.image * (HEADS * (per0 + per1)) + self.pair * (2 * per) + (
                self.layer * HEADS * per0 + self.slot * per + extra)

        def heads0(self, per, extra):
            return self.image * (HEADS * per) + self.pair * (2 * per) + (self.slot * per + extra)

    def each_head(engine, image, layer, prepare, main):
        prepare(At(image, layer, 0, 0))
        main(At(image, layer, 0, 0), At(image, layer, 0, 1), True)
        with engine.Fori(0, HEADS // 2 - 1) as j:
            main(At(image, layer, j, 1), At(image, layer, j + 1, 0), False)
            main(At(image, layer, j + 1, 0), At(image, layer, j + 1, 1), False)
        main(At(image, layer, HEADS // 2 - 1, 1), None, False)

    N_SETUP = 11

    def wait_apart(engine, semaphore, count):
        engine.wait_ge(semaphore, count)
        engine.sem_inc(passed[engine.engine], 1)

    def wait_multiplied(engine, at, c):
        if c < QK_CHUNKS and c >= 0:
            engine.wait_ge(qk_mm, at.phases(4 * QK_CHUNKS, 4 * (c + 1)))
        elif c >= QK_CHUNKS and c < QK_CHUNKS + V_CHUNKS:
            engine.wait_ge(v_mm, at.phases(V_CHUNKS * QT, QT * (c - QK_CHUNKS + 1)))
        else:
            engine.wait_ge(o_mm, at.phases(2 * CT, 4 * (c % CHUNKS - (CHUNKS - O_CHUNKS) + 1)
                                           - (2 * CT if c < 0 else 0)) + start(o_mm))

    def max_steps(layer, t):
        return {4: [0, 1], 5: [2, 3], 6: [4, 5], 7: [6, 7]}.get(t, [])

    MAX_PER = [2 * QT, QT]

    with nc.Block() as block:

        @block.sync
        def _(sp):
            for dst, src in ((group, group_in), (rel, rel_in), (bqk, bqk_in), (scale, scale_in),
                             (bv, bv_in), (bp, bp_in)):
                sp.dma_start(dst[:], src).then_inc(const_in, 16)
            sp.dma_start(qk[:, 0, 0:128], ident_in).then_inc(const_in, 16)
            sp.dma_start(qk[:, 1, :], onehot_in).then_inc(const_in, 16)
            with sp.Fori(0, IMAGES) as image:
                wait_apart(sp, y_sent, image * (16 * CT) + 16)
                sp.dma_start(x[:, :, :], x_in[image]).then_inc(x_in_sem, 16)
                for layer in range(LAYERS):
                    at = At(image, layer)
                    for c in range(CHUNKS):
                        if c == QK_CHUNKS + V_CHUNKS:
                            wait_apart(sp, score_ok, at.phases(HEADS * QT, HEADS * QT))
                        sp.wait_ge(w_hi_ok, at.phases(CHUNKS, c) + start(w_hi_ok))
                        sp.wait_ge(w_lo_ok, at.phases(CHUNKS, c) + start(w_lo_ok))
                        sp.dma_start(raw[:, :, :].rearrange("p a b -> p (a b)"),
                                     w_in[layer, c]).then_inc(raw_in, 16)
                        if c == QK_CHUNKS + V_CHUNKS - 1 and layer == 1:
                            sp.wait_ge(v_ok, at.phases(V_CHUNKS * QT, V_CHUNKS * QT))
                            sp.dma_start(stage[:, :], mask_in).then_inc(stage_in, 16)
                for o in range(CT):
                    wait_apart(sp, o_ok, At(image, 1).phases(2 * CT, 2 * o + 2))
                    sp.dma_start(y_out[image, :, o, :], x[:, o, :]).then_inc(y_sent, 16)
            sp.wait_ge(y_sent, 16 * CT * IMAGES + 16)

        @block.gpsimd
        def _(gp):
            for s, n in ((prob_ok, 2), (pv_done, P_SLOTS), (added, P_SLOTS), (head_done, 2),
                         (sum_mm, 2), (qk_ok, 4), (o_mm, 5), (w_hi_ok, 1), (w_lo_ok, 1),
                         (y_sent, 16)):
                gp.sem_inc(s, n)
            with gp.Fori(0, IMAGES) as image:
                for layer in range(LAYERS):
                    at = At(image, layer)
                    gp.wait_ge(var_ok, at.phases(1, 1))
                    nc.gpsimd.tensor_tensor(rstd[:, :], variance[:, :], power[:, :],
                                            ALU.pow).then_inc(rstd_ok, 1)
                    wait_apart(gp, v_ok, at.phases(V_CHUNKS * QT, V_CHUNKS * QT))
                    nc.gpsimd.memset(max_cols[:, :].bitcast(F32), 0.0).then_inc(cols_zero, 1)
                    def prepare(h):
                        nc.gpsimd.tensor_copy(
                            v_head[h.slot][:, :, :],
                            v[:, :, bass.ds(h.pair * 128 + h.slot * 64, HEAD_DIM)]).then_inc(v_head_ok, 1)

                    def main(h, nxt, first):
                        if nxt is not None:
                            wait_apart(gp, pv_done, h.heads(QT, 0) + start(pv_done))
                            prepare(nxt)
                        total = acc[h.slot]
                        wait_apart(gp, sum_mm, h.heads(1, -1) + start(sum_mm))
                        if layer == 1:
                            nc.gpsimd.memset(total[:, :], 0.0).then_inc(acc_zero, 1)
                            gp.wait_ge(acc_zero, image * HEADS + (h.pair * 2 + (h.slot + 1)))
                        for t in range(QT):
                            a, b = query_span(layer, ORDER[layer][t])
                            if layer == 0 and t == 0:
                                continue
                            gp.wait_ge(prob_ok, h.heads(QT, t + 1) + start(prob_ok))
                            if t > 1 or (layer == 1 and t > 0):
                                gp.wait_ge(added, h.heads(QT, t) + start(added))
                            before = prob[:, 0, :] if layer == 0 and t == 1 else total[:, a:b]
                            nc.gpsimd.tensor_tensor(
                                total[:, a:b], before, prob[:, t % P_SLOTS, 0:b - a],
                                ALU.add).then_inc(added, 2 if layer == 0 and t == 1 else 1)

                    each_head(gp, image, layer, prepare, main)

        @block.scalar
        def _(act):
            def weight_hi(at, c):
                act.wait_ge(raw_in, at.phases(16 * CHUNKS, 16 * (c + 1)))
                wait_multiplied(act, at, c - 2)
                nc.scalar.activation(w_hi[c % 2][:, :, :], raw[:, :, :], ACT.Copy).then_inc(w_hi_ok, 1)

            with act.Fori(0, IMAGES) as image:
                for layer in range(LAYERS):
                    at = At(image, layer)
                    weight_hi(at, 0)
                    for i in range(CT):
                        act.wait_ge(normed, at.phases(CT, i + 1))
                        nc.scalar.activation(a_hi[:, i, :], qk[:, i, :], ACT.Copy).then_inc(a_hi_ok, 1)
                    weight_hi(at, 1)
                    with act.Fori(0, QK_CHUNKS // 2) as i:
                        for s in range(2):
                            act.wait_ge(raw_in, i * 32 + at.phases(16 * CHUNKS, 16 * (s + 3)))
                            act.wait_ge(qk_mm, i * 8 + at.phases(4 * QK_CHUNKS, 4 * (s + 1)))
                            nc.scalar.activation(w_hi[s][:, :, :], raw[:, :, :],
                                                 ACT.Copy).then_inc(w_hi_ok, 1)
                    for c in range(V_CHUNKS):
                        for t in range(QT):
                            n = c * QT + t
                            act.wait_ge(v_mm, at.phases(V_CHUNKS * QT, n + 1))
                            nc.scalar.activation(v[:, t, c * CHUNK:(c + 1) * CHUNK],
                                                 score[:, n // 2 % 2, n % 2, 0:CHUNK],
                                                 ACT.Copy).then_inc(v_ok, 1)
                        if c == 0:
                            weight_hi(at, QK_CHUNKS + 2)

                    def prepare(h, step):
                        rows, where = head_rows(h.slot), pos_rows(h.slot)
                        if step == 0:
                            if layer == 0:
                                nc.scalar.activation(q_rel[rows, :], qk[rows, h.pair, :],
                                                     ACT.Copy).then_inc(q_rel_ok, 1)
                            nc.scalar.activation(q_hi[h.slot][rows, :], qk[rows, h.pair, :],
                                                 ACT.Copy).then_inc(q_hi_ok, 1)
                        elif step == 1:
                            nc.scalar.activation(k_hi[h.slot][rows, :], qk[rows, h.pair + CT, :],
                                                 ACT.Copy).then_inc(k_hi_ok, 1)
                        elif step == 2:
                            nc.scalar.activation(q_max[h.slot][rows, :], qk[rows, h.pair, :],
                                                 ACT.Copy).then_inc(q_max_ok, 1)
                        elif layer == 0:
                            act.wait_ge(pos_mm, h.heads0(1, 1))
                            a = where.start
                            nc.scalar.activation(q_hi[h.slot][a:a + SIDE, :], small_all[a:a + SIDE, :],
                                                 ACT.Copy).then_inc(pos_hi_ok, 1)
                            nc.scalar.activation(
                                q_hi[h.slot][a + SIDE:a + 2 * SIDE, :].rearrange("p (h w) -> p w h", w=SIDE),
                                small_all[a + SIDE:a + 2 * SIDE, :].rearrange("p (w h) -> p w h", h=SIDE),
                                ACT.Copy).then_inc(pos_hi_ok, 1)

                    def main(h, nxt, first):
                        for t in range(QT):
                            a, b = query_span(layer, ORDER[layer][t])
                            act.wait_ge(score_ok, h.heads(QT, t + 1))
                            act.wait_ge(pv_done, h.heads(QT, t + 1 - P_SLOTS) + start(pv_done))
                            act.wait_ge(added, h.heads(QT, t + 1 - P_SLOTS) + start(added))
                            nc.scalar.activation(
                                prob[:, t % P_SLOTS, 0:b - a],
                                score[:, t % 2, :, :].rearrange("p a b -> p (a b)")[:, 0:b - a],
                                ACT.Exp).then_inc(prob_ok, 1)
                            if nxt is not None and t < 4:
                                prepare(nxt, t)

                    def prepare_all(h):
                        act.wait_ge(w_lo_ok, at.phases(CHUNKS, QK_CHUNKS + V_CHUNKS) + start(w_lo_ok))
                        for step in range(4):
                            prepare(h, step)

                    each_head(act, image, layer, prepare_all, main)
                    for i in range(CT):
                        act.wait_ge(head_done, at.phases(HEADS, HEADS) + start(head_done))
                        if layer == 0:
                            nc.scalar.activation(a_hi[:, i, :], qk[:, i, :], ACT.Identity,
                                                 bias=bv[:, i:i + 1]).then_inc(o_hi_ok, 1)
                        else:
                            nc.scalar.activation(a_hi[:, i, :], qk[:, i, :], ACT.Copy).then_inc(o_hi_ok, 1)
                        if i in (0, 1):
                            weight_hi(at, QK_CHUNKS + V_CHUNKS + i)
                    weight_hi(at, CHUNKS - 1)

        @block.vector
        def _(dve):
            def weight_lo(at, c, more=0, s=None):
                dve.wait_ge(w_hi_ok, more + at.phases(CHUNKS, c + 1) + start(w_hi_ok))
                s = c % 2
                nc.vector.tensor_tensor(w_lo[s][:, :, :], raw[:, :, :], w_hi[s][:, :, :].bitcast(F32),
                                        ALU.subtract).then_inc(w_lo_ok, 1)

            nc.vector.memset(ones[:, :], 1.0).then_inc(const_ok, 1)
            nc.vector.memset(power[:, :], -0.5).then_inc(const_ok, 1)
            for s in range(2):
                nc.vector.memset(k_lo[s][pos_rows(s), :].bitcast(F32), 0.0).then_inc(const_ok, 1)
                nc.vector.memset(q_max[s][pos_rows(s), :].bitcast(F32), 0.0).then_inc(const_ok, 1)
            dve.wait_ge(const_ok, 6)
            for s in range(2):
                r = max_row(s)
                nc.vector.memset(k_lo[s][r:r + 1, :].bitcast(F32), -1.0).then_inc(const_ok, 1)
            dve.wait_ge(const_in, 16 * 8)
            nc.vector.tensor_copy(ident[:, :], qk[:, 0, 0:128]).then_inc(const_ok, 1)
            for s in range(2):
                nc.vector.tensor_copy(k_hi[s][pos_rows(s), :], qk[pos_rows(s), 1, :]).then_inc(const_ok, 1)
            dve.wait_ge(const_ok, N_SETUP)
            with dve.Fori(0, IMAGES) as image:
                for layer in range(LAYERS):
                    at = At(image, layer)
                    if layer == 0:
                        dve.wait_ge(x_in_sem, image * 16 + 16)
                    else:
                        dve.wait_ge(o_ok, at.phases(2 * CT, 0))
                    for i in range(CT):
                        for half in range(2):
                            nc.vector.bn_stats(bn[:, i, half, :], x[:, i, half * HALF:(half + 1) * HALF])\
                                .then_inc(bn_ok, 1)
                    wait_apart(dve, bn_ok, at.phases(2 * CT, 2 * CT))
                    for i in range(CT):
                        nc.vector.bn_aggr(mean_var[:, i, :], bn[:, i, :, :].rearrange("p a b -> p (a b)"))\
                            .then_inc(mv_ok, 1)
                    dve.wait_ge(gsum_ok, at.phases(1, 1))
                    nc.vector.tensor_copy(group_mv[:, :, :],
                                          small[:, 0, 0:2 * CT].rearrange("p (i k) -> p i k", k=2))\
                        .then_inc(gmv_ok, 1)
                    dve.wait_ge(gmv_ok, at.phases(1, 1))
                    dve.wait_ge(mv_ok, at.phases(CT, CT))
                    nc.vector.tensor_tensor(shift2[:, 0, :], mean_var[:, :, 0], group_mv[:, :, 0],
                                            ALU.subtract).then_inc(shift_ok, 1)
                    dve.wait_ge(shift_ok, at.phases(1, 1))
                    nc.vector.tensor_tensor(shift2[:, 1, :], shift2[:, 0, :], shift2[:, 0, :],
                                            ALU.mult).then_inc(shift2_ok, 1)
                    dve.wait_ge(gshift_ok, at.phases(1, 1))
                    nc.vector.scalar_tensor_tensor(variance[:, :], small[:, 1, 0:CT], EPS,
                                                   group_mv[:, :, 1], ALU.add, ALU.add).then_inc(var_ok, 1)
                    weight_lo(at, 0)
                    dve.wait_ge(rstd_ok, at.phases(1, 1))
                    for i in range(CT):
                        nc.vector.tensor_scalar(qk[:, i, :], x[:, i, :], group_mv[:, i, 0:1],
                                                rstd[:, i:i + 1], ALU.subtract, ALU.mult).then_inc(normed, 1)
                    for i in range(CT):
                        dve.wait_ge(a_hi_ok, at.phases(CT, i + 1))
                        nc.vector.tensor_tensor(a_lo[:, i, :], qk[:, i, :], a_hi[:, i, :].bitcast(F32),
                                                ALU.subtract).then_inc(a_lo_ok, 1)
                    weight_lo(at, 1)
                    with dve.Fori(0, QK_CHUNKS // 2) as i:
                        for s in range(2):
                            for k in range(4):
                                n, o = 4 * s + k, 2 * s + k // 2
                                dve.wait_ge(qk_mm, i * 8 + at.phases(4 * QK_CHUNKS, n + 1))
                                tile = i * 4 + o
                                dst = qk[:, tile, (k % 2) * HALF:(k % 2 + 1) * HALF]
                                src = score[:, n // 2 % 2, n % 2, :]
                                if layer == 0:
                                    nc.vector.tensor_scalar(dst, src, bqk[:, bass.ds(tile, 1)],
                                                            scale[:, bass.ds(tile, 1)],
                                                            ALU.add, ALU.mult).then_inc(qk_ok, 1)
                                else:
                                    nc.vector.tensor_scalar(dst, src, scale[:, bass.ds(tile, 1)], None,
                                                            ALU.mult).then_inc(qk_ok, 1)
                            weight_lo(at, s + 2, i * 2)
                    weight_lo(at, QK_CHUNKS + 2)
                    if layer == 1:
                        wait_apart(dve, stage_in, image * 16 + 16)
                        for s in range(2):
                            nc.vector.tensor_copy(q_hi[s][pos_rows(s), :], stage[pos_rows(s), :])\
                                .then_inc(mask_ok, 1)
                            nc.vector.memset(q_lo[s][pos_rows(s), :].bitcast(F32), 0.0)\
                                .then_inc(mask_ok, 1)

                    def prepare(h, part):
                        rows, where, s = head_rows(h.slot), pos_rows(h.slot), h.slot
                        if part == 0:
                            dve.wait_ge(q_hi_ok, h.heads(1, 1))
                            nc.vector.tensor_tensor(q_lo[s][rows, :], qk[rows, h.pair, :],
                                                    q_hi[s][rows, :].bitcast(F32),
                                                    ALU.subtract).then_inc(q_lo_ok, 1)
                            dve.wait_ge(k_hi_ok, h.heads(1, 1))
                            nc.vector.tensor_tensor(k_lo[s][rows, :], qk[rows, h.pair + CT, :],
                                                    k_hi[s][rows, :].bitcast(F32),
                                                    ALU.subtract).then_inc(k_lo_ok, 1)
                        if part == 1 and layer == 0:
                            a = where.start
                            dve.wait_ge(pos_hi_ok, h.heads0(2, 1))
                            nc.vector.tensor_tensor(q_lo[s][a:a + SIDE, :], small_all[a:a + SIDE, :],
                                                    q_hi[s][a:a + SIDE, :].bitcast(F32),
                                                    ALU.subtract).then_inc(pos_lo_ok, 1)
                            dve.wait_ge(pos_hi_ok, h.heads0(2, 2))
                            a += SIDE
                            nc.vector.tensor_tensor(
                                q_lo[s][a:a + SIDE, :].rearrange("p (h w) -> p w h", w=SIDE),
                                small_all[a:a + SIDE, :].rearrange("p (w h) -> p w h", h=SIDE),
                                q_hi[s][a:a + SIDE, :].rearrange("p (h w) -> p w h", w=SIDE).bitcast(F32),
                                ALU.subtract).then_inc(pos_lo_ok, 1)
                        if part == 2:
                            n = 0
                            for t in range(QT):
                                for half in range(2 if layer == 0 else 1):
                                    dve.wait_ge(max_mm, h.heads2(*MAX_PER, n + 1))
                                    size = HALF if layer == 0 else key_span(t)[1] - key_span(t)[0]
                                    nc.vector.reduce_max(max_part[:, t, half:half + 1],
                                                         small[:, n % 2, 0:size], AX.X)\
                                        .then_inc(max_part_ok, 1)
                                    n += 1
                            dve.wait_ge(max_part_ok, h.heads2(*MAX_PER, n))
                            dst = max_cols[:, 64:].rearrange("p (t c) -> p t c", c=128)[:, :, 0]
                            if layer == 0:
                                nc.vector.tensor_tensor(dst, max_part[:, :, 0], max_part[:, :, 1],
                                                        ALU.max).then_inc(max_cols_ok, 1)
                            else:
                                nc.vector.tensor_copy(dst, max_part[:, :, 0]).then_inc(max_cols_ok, 1)
                            dve.wait_ge(max_row_mm, h.heads(1, 1))
                            r = max_row(s)
                            nc.vector.tensor_copy(q_max[s][r:r + 1, :], small_all[r:r + 1, :])\
                                .then_inc(max_row_ok, 1)

                    def normalise(h):
                        dve.wait_ge(sum_mm, h.heads(1, 1) + start(sum_mm))
                        nc.vector.reciprocal(recip[:, :], small[:, 0, :]).then_inc(recip_ok, 1)
                        dve.wait_ge(recip_ok, h.heads(1, 1))
                        rows = head_rows(h.slot)
                        for half in range(2):
                            part = head_rows(half)
                            last = nc.vector.tensor_tensor(
                                qk[rows, h.pair, half * HALF:(half + 1) * HALF],
                                head_out[part, h.slot, :], recip[part, :], ALU.mult)
                            last.then_inc(*((head_done, 1) if half else (recip_used, 1)))

                    def prepare_all(h):
                        dve.wait_ge(cols_zero, at.phases(1, 1))
                        for part in range(3):
                            prepare(h, part)

                    def main(h, nxt, first):
                        if nxt is not None:
                            prepare(nxt, 0)
                        if not first:
                            before = At(image, layer, h.pair if h.slot else h.pair - 1, 1 - h.slot)
                            normalise(before)
                        if nxt is not None:
                            prepare(nxt, 1)
                            prepare(nxt, 2)
                        else:
                            normalise(h)

                    each_head(dve, image, layer, prepare_all, main)
                    for i in range(CT):
                        dve.wait_ge(o_hi_ok, at.phases(CT, i + 1))
                        if layer == 0:
                            nc.vector.scalar_tensor_tensor(a_lo[:, i, :], qk[:, i, :], bv[:, i:i + 1],
                                                           a_hi[:, i, :].bitcast(F32), ALU.add,
                                                           ALU.subtract).then_inc(o_lo_ok, 1)
                        else:
                            nc.vector.tensor_tensor(a_lo[:, i, :], qk[:, i, :], a_hi[:, i, :].bitcast(F32),
                                                    ALU.subtract).then_inc(o_lo_ok, 1)
                        if i in (0, 1):
                            weight_lo(at, QK_CHUNKS + V_CHUNKS + i)
                    for n in range(2 * CT):
                        o, half = n // 2, n % 2
                        dve.wait_ge(o_mm, at.phases(2 * CT, n + 1) + start(o_mm))
                        dst = x[:, o, half * HALF:(half + 1) * HALF]
                        src = score[:, n // 2 % 2, n % 2, :]
                        if layer == 0:
                            nc.vector.scalar_tensor_tensor(dst, src, bp[:, o:o + 1], dst, ALU.add,
                                                           ALU.add).then_inc(o_ok, 1)
                        else:
                            nc.vector.tensor_tensor(dst, src, dst, ALU.add).then_inc(o_ok, 1)
                        if n == 3:
                            weight_lo(at, CHUNKS - 1)

        @block.tensor
        def _(pe):
            def split_product(out, w, a, first, last):
                nc.tensor.matmul(out, w[0], a[0], start=first, stop=False)
                nc.tensor.matmul(out, w[0], a[1], start=False, stop=False)
                return nc.tensor.matmul(out, w[1], a[0], start=False, stop=last)

            pe.wait_ge(const_ok, N_SETUP)
            with pe.Fori(0, IMAGES) as image:
                for layer in range(LAYERS):
                    at = At(image, layer)
                    pe.wait_ge(mv_ok, at.phases(CT, CT))

                    def averages(bank, stats, width, done):
                        for j in range(CT):
                            from_tiles = [(n, i + j // GROUP_SPAN * GROUP_SPAN)
                                          for n, (i, k) in enumerate(blocks) if k == j % GROUP_SPAN]
                            for k, (n, i) in enumerate(from_tiles):
                                last = nc.tensor.matmul(small[:, bank, j * width:(j + 1) * width],
                                                        group[:, n, :], stats(i), start=(k == 0),
                                                        stop=(k == len(from_tiles) - 1))
                        last.then_inc(done, 1)

                    averages(0, lambda i: mean_var[:, i, :], 2, gsum_ok)
                    pe.wait_ge(shift2_ok, at.phases(1, 1))
                    averages(1, lambda i: shift2[:, 1, i:i + 1], 1, gshift_ok)
                    wait_apart(pe, a_lo_ok, at.phases(CT, CT))
                    with pe.Fori(0, QK_CHUNKS // 2) as i:
                        for s in range(2):
                            pe.wait_ge(w_hi_ok, i * 2 + at.phases(CHUNKS, s + 1) + start(w_hi_ok))
                            pe.wait_ge(w_lo_ok, i * 2 + at.phases(CHUNKS, s + 1) + start(w_lo_ok))
                            for k in range(4):
                                n, cols = 4 * s + k, slice(k // 2 * 128, k // 2 * 128 + 128)
                                half = slice(k % 2 * HALF, (k % 2 + 1) * HALF)
                                pe.wait_ge(qk_ok, i * 8 + at.phases(4 * QK_CHUNKS, n - 3) + start(qk_ok))
                                for c in range(CT):
                                    last = split_product(score[:, n // 2 % 2, n % 2, :],
                                                         (w_hi[s][:, c, cols], w_lo[s][:, c, cols]),
                                                         (a_hi[:, c, half], a_lo[:, c, half]),
                                                         c == 0, c == CT - 1)
                                last.then_inc(qk_mm, 1)
                    for c in range(V_CHUNKS):
                        chunk, s = QK_CHUNKS + c, c % 2
                        pe.wait_ge(w_lo_ok, at.phases(CHUNKS, chunk + 1) + start(w_lo_ok))
                        for t in range(QT):
                            n = c * QT + t
                            if n < 4:
                                pe.wait_ge(qk_ok, at.phases(4 * QK_CHUNKS, 4 * QK_CHUNKS - 3 + n) + start(qk_ok))
                            else:
                                pe.wait_ge(v_ok, at.phases(V_CHUNKS * QT, n - 3))
                            tok = slice(t * 128, (t + 1) * 128)
                            for i in range(CT):
                                last = split_product(score[:, n // 2 % 2, n % 2, 0:CHUNK],
                                                     (a_hi[:, i, tok], a_lo[:, i, tok]),
                                                     (w_hi[s][:, i, :], w_lo[s][:, i, :]),
                                                     i == 0, i == CT - 1)
                            last.then_inc(v_mm, 1)

                    def position(h):
                        rows, a = head_rows(h.slot), pos_rows(h.slot).start
                        wait_apart(pe, q_rel_ok, h.heads0(1, 1))
                        by_row = q_rel[rows, :].rearrange("p (h w) -> p h w", w=SIDE)
                        for i in range(SIDE):
                            window = slice(SIDE - 1 - i, 2 * SIDE - 1 - i)
                            nc.tensor.matmul(small_all[a:a + SIDE, i * SIDE:(i + 1) * SIDE],
                                             rel[rows, 0, window], by_row[:, i, :], start=True, stop=True)
                            last = nc.tensor.matmul(small_all[a + SIDE:a + 2 * SIDE, i * SIDE:(i + 1) * SIDE],
                                                    rel[rows, 1, window], by_row[:, :, i],
                                                    start=True, stop=True)
                        last.then_inc(pos_mm, 1)

                    def maximum(h, tiles):
                        s = h.slot
                        for t in tiles:
                            if t == 0:
                                pe.wait_ge(q_hi_ok, h.heads(1, 1))
                                pe.wait_ge(k_hi_ok, h.heads(1, 1))
                                if layer == 0:
                                    pe.wait_ge(pos_lo_ok, h.heads0(2, 2))
                            for half in range(2 if layer == 0 else 1):
                                n = 2 * t + half if layer == 0 else t
                                a, b = (half * HALF, (half + 1) * HALF) if layer == 0 else key_span(t)
                                if n >= 2:
                                    pe.wait_ge(max_part_ok, h.heads2(*MAX_PER, n - 1))
                                nc.tensor.matmul(small[:, n % 2, 0:b - a],
                                                 q_hi[s][:, t * 128:(t + 1) * 128], k_hi[s][:, a:b],
                                                 start=True, stop=True).then_inc(max_mm, 1)

                    def maximum_row(h):
                        pe.wait_ge(max_cols_ok, h.heads(1, 1))
                        for t in range(QT):
                            a = t * 128 + 64 * h.slot
                            last = nc.tensor.matmul(small_all[:, t * 128:(t + 1) * 128],
                                                    max_cols[:, a:a + 128], ident[:, :],
                                                    start=True, stop=True)
                        last.then_inc(max_row_mm, 1)

                    def scores(h, step):
                        s, t = h.slot, ORDER[layer][step]
                        a, b = query_span(layer, t)
                        pe.wait_ge(prob_ok, h.heads(QT, step - 1) + start(prob_ok))
                        keys = slice(t * 128, (t + 1) * 128)
                        pieces = [(a, a + HALF), (a + HALF, b)] if b - a > HALF else [(a, b)]
                        if step == 0:
                            pe.wait_ge(q_lo_ok, h.heads(1, 1))
                        for w, x_, first, stop in ((k_hi, q_hi, True, False), (k_hi, q_lo, False, False),
                                                   (k_lo, q_max, False, True)):
                            if step == 0 and stop:
                                pe.wait_ge(k_lo_ok, h.heads(1, 1))
                                pe.wait_ge(q_max_ok, h.heads(1, 1))
                                pe.wait_ge(max_row_ok, h.heads(1, 1))
                            for n, (p, q) in enumerate(pieces):
                                last = nc.tensor.matmul(score[:, step % 2, n, 0:q - p], w[s][:, keys],
                                                        x_[s][:, p:q], start=first, stop=stop)
                        last.then_inc(score_ok, 1)

                    def values(h, step):
                        s = h.slot
                        steps = [step] if layer == 0 else [step - 1, step]
                        if step == 0 or (layer == 1 and step == 1):
                            pe.wait_ge(v_head_ok, h.heads(1, 1))
                            pe.wait_ge(head_done, h.heads(1, -1) + start(head_done))
                        pe.wait_ge(prob_ok, h.heads(QT, step + 1) + start(prob_ok))
                        for u in steps:
                            t = ORDER[layer][u]
                            a, b = query_span(layer, t)
                            for half in range(2):
                                p, q = max(a, half * HALF), min(b, (half + 1) * HALF)
                                if p >= q:
                                    continue
                                first = (u == 0 or (layer == 1 and u == 1))
                                last_u = QT - 1 if layer == 0 else QT - 1
                                out = head_out[head_rows(half), s, p - half * HALF:q - half * HALF]
                                last = nc.tensor.matmul(out, v_head[s][:, t, :],
                                                        prob[:, u % P_SLOTS, p - a:q - a],
                                                        start=first, stop=(u == last_u),
                                                        skip_group_check=(layer == 1))
                        last.then_inc(pv_done, len(steps))

                    def sums(h):
                        pe.wait_ge(added, h.heads(QT, QT) + start(added))
                        for half in range(2):
                            last = nc.tensor.matmul(small[head_rows(half), 0, :], ones[:, :],
                                                    acc[h.slot][:, half * HALF:(half + 1) * HALF],
                                                    start=True, stop=True)
                        last.then_inc(sum_mm, 1)

                    def prepare(h):
                        pe.wait_ge(v_ok, at.phases(V_CHUNKS * QT, V_CHUNKS * QT))
                        if layer == 0:
                            position(h)
                        else:
                            pe.wait_ge(mask_ok, image * 4 + 4)
                        maximum(h, range(QT))
                        maximum_row(h)

                    def main(h, nxt, first):
                        before = None
                        if not first:
                            before = At(image, layer, h.pair if h.slot else h.pair - 1, 1 - h.slot)
                        for t in range(QT):
                            scores(h, t)
                            if layer == 0:
                                if t > 0:
                                    values(h, t - 1)
                                elif before is not None:
                                    values(before, QT - 1)
                            elif t % 2 == 0:
                                if t > 0:
                                    values(h, t - 1)
                                elif before is not None:
                                    values(before, QT - 1)
                            if t == 1 and before is not None:
                                sums(before)
                            if nxt is None:
                                continue
                            if t == 2 and layer == 0:
                                if before is not None:
                                    pe.wait_ge(head_done, before.heads(1, 1) + start(head_done))
                                pe.wait_ge(max_row_ok, h.heads(1, 1))
                                position(nxt)
                            if t == 4 and layer == 1 and before is not None:
                                pe.wait_ge(head_done, before.heads(1, 1) + start(head_done))
                            maximum(nxt, max_steps(layer, t))
                        if nxt is not None:
                            maximum_row(nxt)
                        else:
                            values(h, QT - 1)
                            pe.wait_ge(head_done, before.heads(1, 1) + start(head_done))
                            sums(h)

                    each_head(pe, image, layer, prepare, main)
                    for n in range(2 * CT):
                        o, half = n // 2, n % 2
                        chunk = QK_CHUNKS + V_CHUNKS + o // 2
                        s, cols = chunk % 2, slice(o % 2 * 128, o % 2 * 128 + 128)
                        if n % 4 == 0:
                            pe.wait_ge(w_lo_ok, at.phases(CHUNKS, chunk + 1) + start(w_lo_ok))
                        if n >= 4:
                            pe.wait_ge(o_ok, at.phases(2 * CT, n - 3))
                        h = slice(half * HALF, (half + 1) * HALF)
                        for c in range(CT):
                            if n == 0:
                                pe.wait_ge(o_lo_ok, at.phases(CT, c + 1))
                            last = split_product(score[:, n // 2 % 2, n % 2, :],
                                                 (w_hi[s][:, c, cols], w_lo[s][:, c, cols]),
                                                 (a_hi[:, c, h], a_lo[:, c, h]), c == 0, c == CT - 1)
                        last.then_inc(o_mm, 1)
    

def kernel(**inputs):
    import numpy as np
    import concourse.bacc as bacc
    from concourse.bass_utils import run_bass_kernel_spmd

    f32 = np.float32

    def tiles(a):
        a = np.asarray(a)
        return np.ascontiguousarray(a.reshape(CT, 128, -1).transpose(1, 0, 2))

    def vector_tiles(a):
        return np.ascontiguousarray(np.asarray(a).reshape(-1, 128).T)

    def chunks(w):
        w = tiles(w)
        return [w[:, :, n:n + CHUNK].reshape(128, CT * CHUNK) for n in range(0, w.shape[2], CHUNK)]

    x = np.asarray(inputs["x"])
    x_t = x.reshape(IMAGES, TOKENS, CT, 128).transpose(0, 3, 2, 1)
    qkv = np.asarray(inputs["L1_conv_qkv_w"])
    weights = np.stack([
        np.stack(sum((chunks(inputs[f"L0_conv_W{n}"]) for n in "qkvp"), [])),
        np.stack(chunks(qkv.T) + chunks(np.asarray(inputs["L1_conv_out_w"]).T)),
    ])
    rel = np.stack([np.asarray(inputs[f"L0_conv_rel_{n}"])[::-1].T for n in "hw"], axis=1)
    token = np.arange(TOKENS)
    line = np.arange(SIDE)
    onehot = np.concatenate([token // SIDE == line[:, None], token % SIDE == line[:, None]]).astype(f32)
    near = np.clip(line, RADIUS, SIDE - 1 - RADIUS)
    far = np.abs(near[None, :] - line[:, None]) > RADIUS
    mask = np.where(np.concatenate([far[:, token // SIDE], far[:, token % SIDE]]), f32(-2.0 ** 100), f32(0))
    channel = np.arange(GROUP_SPAN * 128)
    same = (channel[:, None] // GROUP == channel[None, :] // GROUP) * (1.0 / GROUP)
    group = np.stack([same[i * 128:(i + 1) * 128, j * 128:(j + 1) * 128] for i, j in group_blocks()], axis=1)
    scale = np.ones((128, QK_TILES), f32)
    scale[:, CT:] = HEAD_DIM ** -0.5
    arrays = {
        "x_t": x_t,
        "weights": weights,
        "bias_qk": np.concatenate([vector_tiles(inputs[f"L0_conv_b{n}"]) for n in "qk"], axis=1),
        "scale_qk": scale,
        "bias_v": vector_tiles(inputs["L0_conv_bv"]),
        "bias_out": vector_tiles(inputs["L0_conv_bp"]),
        "rel": np.concatenate([rel, rel]),
        "onehot": np.concatenate([onehot, onehot]),
        "mask": np.concatenate([mask, mask]).astype(f32),
        "group": group.astype(f32),
        "ident": np.eye(128, dtype=f32),
    }
    arrays = {k: np.ascontiguousarray(a) for k, a in arrays.items()}
    nc = bacc.Bacc("TRN2", target_bir_lowering=False, num_devices=1)
    args = [nc.dram_tensor(k, a.shape, mybir.dt.from_np(a.dtype), kind="ExternalInput").ap()
            for k, a in arrays.items()]
    y = nc.dram_tensor("y_t", (IMAGES, 128, CT, TOKENS), F32, kind="ExternalOutput").ap()
    build(nc, *args, y)
    r = run_bass_kernel_spmd(nc, [arrays], core_ids=[0])
    y_t = np.asarray(r.results[0]["y_t"])
    return np.ascontiguousarray(y_t.transpose(0, 3, 2, 1)).reshape(x.shape)
```

```python
import concourse.bass as bass
from concourse import mybir

F32 = mybir.dt.float32
F32R = mybir.dt.float32r
ALU = mybir.AluOpType
ACT = mybir.ActivationFunctionType
AX = mybir.AxisListType

IMAGES, SIDE, CHANNELS, HEADS, LAYERS = 4, 32, 768, 12, 2
TOKENS = SIDE * SIDE
HEAD_DIM = CHANNELS // HEADS
CT = CHANNELS // 128
QT = TOKENS // 128
HALF = TOKENS // 2
CHUNK = 256
QK_CHUNKS, V_CHUNKS, O_CHUNKS = 6, 3, 3
CHUNKS = QK_CHUNKS + V_CHUNKS + O_CHUNKS
QK_TILES = 2 * CT
REL = 2 * SIDE - 1
GROUP = CHANNELS // 32
GROUP_SPAN = 3
EPS = 1e-5
REACH, RADIUS = 7, 3
P_SLOTS = 4
ORDER = [[0, 1, 2, 3, 4, 5, 6, 7], [0, 7, 1, 6, 2, 5, 3, 4]]


def centre(i):
    return min(max(i, RADIUS), SIDE - 1 - RADIUS)


def query_span(layer, key_tile):
    if layer == 0:
        return 0, TOKENS
    rows = range(4 * key_tile, 4 * key_tile + 4)
    near = [i for i in range(SIDE) if any(abs(centre(i) - r) <= RADIUS for r in rows)]
    return near[0] * SIDE, (near[-1] + 1) * SIDE


def key_span(query_tile):
    c = [centre(i) for i in range(4 * query_tile, 4 * query_tile + 4)]
    return (min(c) - RADIUS) * SIDE, (max(c) + RADIUS + 1) * SIDE


def group_blocks():
    return [(i, j) for j in range(GROUP_SPAN) for i in range(GROUP_SPAN) if abs(i - j) <= 1]


class Memory:

    def __init__(self, nc, at):
        self.nc, self.at = nc, at

    def put(self, name, shape, dtype=F32):
        size = 4
        for n in shape[1:]:
            size *= n
        t = self.nc.alloc_sbuf_tensor_at(name, shape, dtype, offset=self.at)
        self.at += (size + 31) // 32 * 32
        return t


def build(nc, x_in, w_in, bqk_in, scale_in, bv_in, bp_in, rel_in, onehot_in, mask_in, group_in,
          ident_in, y_out):
    blocks = group_blocks()
    m = Memory(nc, (nc.sbuf_base + 31) // 32 * 32)
    x = m.put("x", [128, CT, TOKENS])
    qk = m.put("qk", [128, QK_TILES, TOKENS])
    v = m.put("v", [128, QT, CHANNELS])
    k_hi = [m.put(f"k_hi{s}", [128, TOKENS], F32R) for s in range(2)]
    k_lo = [m.put(f"k_lo{s}", [128, TOKENS], F32R) for s in range(2)]
    q_max = [m.put(f"q_max{s}", [128, TOKENS], F32R) for s in range(2)]
    w_hi0 = m.put("w_hi0", [128, CT, CHUNK], F32R)
    w_lo0 = m.put("w_lo0", [128, CT, CHUNK], F32R)
    group = m.put("group", [128, len(blocks), 128])
    ident = m.put("ident", [128, 128], F32R)
    ones = m.put("ones", [128, 64])
    rel = m.put("rel", [128, 2, REL])
    bqk = m.put("bqk", [128, QK_TILES])
    scale = m.put("scale", [128, QK_TILES])
    bv = m.put("bv", [128, CT])
    bp = m.put("bp", [128, CT])
    bn = m.put("bn", [128, CT, 2, 6])
    mean_var = m.put("mean_var", [128, CT, 2])
    group_mv = m.put("group_mv", [128, CT, 2])
    shift2 = m.put("shift2", [128, 2, CT])
    variance = m.put("variance", [128, CT])
    power = m.put("power", [128, CT])
    rstd = m.put("rstd", [128, CT])
    max_part = m.put("max_part", [128, 2 * QT])
    shared = m.at
    q_hi = [m.put(f"q_hi{s}", [128, TOKENS], F32R) for s in range(2)]
    q_lo = [m.put(f"q_lo{s}", [128, TOKENS], F32R) for s in range(2)]
    end = m.at
    m.at = shared
    w_hi1 = m.put("w_hi1", [128, CT, CHUNK], F32R)
    w_lo1 = m.put("w_lo1", [128, CT, CHUNK], F32R)
    raw = m.put("raw", [128, CT, CHUNK])
    m.at = max(m.at, end)
    w_hi, w_lo = [w_hi0, w_hi1], [w_lo0, w_lo1]
    shared = m.at
    a_hi = m.put("a_hi", [128, CT, TOKENS], F32R)
    a_lo = m.put("a_lo", [128, CT, TOKENS], F32R)
    assert m.at <= nc.sbuf_usable_end
    m.at = shared
    prob = m.put("prob", [128, P_SLOTS, TOKENS])
    acc = [m.put(f"acc{s}", [128, TOKENS]) for s in range(2)]
    v_head = [m.put(f"v_head{s}", [128, QT, HEAD_DIM]) for s in range(2)]
    q_rel = m.put("q_rel", [128, TOKENS])
    max_cols = m.put("max_cols", [128, 64 + QT * 128], F32R)
    sums = m.put("sums", [128, HALF])
    recip = m.put("recip", [128, HALF])
    stage = m.put("stage", [128, TOKENS])

    score = nc.alloc_psum_tensor("score", [128, 2, 2, HALF], F32)
    small = nc.alloc_psum_tensor("small", [128, 2, HALF], F32)
    head_out = nc.alloc_psum_tensor("head_out", [128, 2, HALF], F32)
    small_all = small[:, :, :].rearrange("p a b -> p (a b)")

    def sem(name):
        return nc.alloc_semaphore(name)

    const_in, const_ok, stage_in = sem("const_in"), sem("const_ok"), sem("stage_in")
    x_in_sem, raw_in, y_sent = sem("x_in"), sem("raw_in"), sem("y_sent")
    bn_ok, mv_ok, gsum_ok, gmv_ok, shift_ok, shift2_ok = (sem(n) for n in (
        "bn_ok", "mv_ok", "gsum_ok", "gmv_ok", "shift_ok", "shift2_ok"))
    gshift_ok, var_ok, rstd_ok, normed = (sem(n) for n in ("gshift_ok", "var_ok", "rstd_ok", "normed"))
    a_hi_ok, a_lo_ok, w_hi_ok, w_lo_ok = (sem(n) for n in ("a_hi_ok", "a_lo_ok", "w_hi_ok", "w_lo_ok"))
    qk_mm, qk_ok, v_mm, v_ok, o_mm, o_ok = (sem(n) for n in (
        "qk_mm", "qk_ok", "v_mm", "v_ok", "o_mm", "o_ok"))
    mask_ok, cols_zero, o_hi_ok, o_lo_ok = (sem(n) for n in ("mask_ok", "cols_zero", "o_hi_ok", "o_lo_ok"))
    q_rel_ok, v_head_ok, q_hi_ok, k_hi_ok, q_max_ok, q_lo_ok, k_lo_ok = (sem(n) for n in (
        "q_rel_ok", "v_head_ok", "q_hi_ok", "k_hi_ok", "q_max_ok", "q_lo_ok", "k_lo_ok"))
    pos_mm, pos_hi_ok, pos_lo_ok = sem("pos_mm"), sem("pos_hi_ok"), sem("pos_lo_ok")
    max_mm, max_part_ok, max_cols_ok, max_row_mm, max_row_ok = (sem(n) for n in (
        "max_mm", "max_part_ok", "max_cols_ok", "max_row_mm", "max_row_ok"))
    max_row2_ok, sums_out = sem("max_row2_ok"), sem("sums_out")
    score_ok, prob_ok, pv_done, added, sum_mm, recip_ok, head_done = (sem(n) for n in (
        "score_ok", "prob_ok", "pv_done", "added", "sum_mm", "recip_ok", "head_done"))
    acc_zero, recip_used = sem("acc_zero"), sem("recip_used")
    passed = {e.engine: sem(f"passed_{n}") for n, e in (
        ("tensor", nc.tensor), ("vector", nc.vector), ("gpsimd", nc.gpsimd), ("sync", nc.sync))}

    START = {id(prob_ok): 2, id(pv_done): P_SLOTS, id(added): P_SLOTS, id(head_done): 2,
             id(sum_mm): 2, id(recip_ok): 1, id(qk_ok): 4, id(o_mm): 5, id(w_hi_ok): 1, id(w_lo_ok): 1}

    def start(s):
        return START.get(id(s), 0)

    def head_rows(s):
        return slice(64 * s, 64 * s + 64)

    def pos_rows(s):
        return slice(64 - 64 * s, 128 - 64 * s)

    def max_row(s):
        return 64 - 64 * s

    class At:

        def __init__(self, image, layer, pair=None, slot=None):
            self.image, self.layer, self.pair, self.slot = image, layer, pair, slot

        def phases(self, per, extra):
            return self.image * (2 * per) + (self.layer * per + extra)

        def layer0(self, per, extra):
            return self.image * per + extra

        def heads(self, per, extra):
            return self.image * (2 * HEADS * per) + self.pair * (2 * per) + (
                (self.layer * HEADS + self.slot) * per + extra)

        def heads2(self, per0, per1, extra):
            per = per1 if self.layer else per0
            return self.image * (HEADS * (per0 + per1)) + self.pair * (2 * per) + (
                self.layer * HEADS * per0 + self.slot * per + extra)

        def heads0(self, per, extra):
            return self.image * (HEADS * per) + self.pair * (2 * per) + (self.slot * per + extra)

    def each_head(engine, image, layer, prepare, main):
        prepare(At(image, layer, 0, 0))
        main(At(image, layer, 0, 0), At(image, layer, 0, 1), True)
        with engine.Fori(0, HEADS // 2 - 1) as j:
            main(At(image, layer, j, 1), At(image, layer, j + 1, 0), False)
            main(At(image, layer, j + 1, 0), At(image, layer, j + 1, 1), False)
        main(At(image, layer, HEADS // 2 - 1, 1), None, False)

    N_SETUP = 11

    def wait_apart(engine, semaphore, count):
        engine.wait_ge(semaphore, count)
        engine.sem_inc(passed[engine.engine], 1)

    def wait_multiplied(engine, at, c):
        if c < QK_CHUNKS and c >= 0:
            engine.wait_ge(qk_mm, at.phases(4 * QK_CHUNKS, 4 * (c + 1)))
        elif c >= QK_CHUNKS and c < QK_CHUNKS + V_CHUNKS:
            engine.wait_ge(v_mm, at.phases(V_CHUNKS * QT, QT * (c - QK_CHUNKS + 1)))
        else:
            engine.wait_ge(o_mm, at.phases(2 * CT, 4 * (c % CHUNKS - (CHUNKS - O_CHUNKS) + 1)
                                           - (2 * CT if c < 0 else 0)) + start(o_mm))

    MAX_IN_STEP = [[0, 0, 0, 2, 3, 3, 4, 4], [0, 0, 0, 1, 2, 1, 2, 2]]
    MAX_AFTER = {0: [], 1: [2], 2: [0, 2], 3: [0, 1, 2], 4: [0, 1, 2, 2]}

    def max_turn(layer, t, part):
        n = sum(MAX_IN_STEP[layer][:t])
        after = [1, 2] if t == 3 and layer == 0 else MAX_AFTER[MAX_IN_STEP[layer][t]]
        return [n + k for k, p in enumerate(after) if p == part]

    MAX_PER = [2 * QT, QT]

    with nc.Block() as block:

        @block.sync
        def _(sp):
            for dst, src in ((group, group_in), (rel, rel_in), (bqk, bqk_in), (scale, scale_in),
                             (bv, bv_in), (bp, bp_in)):
                sp.dma_start(dst[:], src).then_inc(const_in, 16)
            sp.dma_start(qk[:, 0, 0:128], ident_in).then_inc(const_in, 16)
            sp.dma_start(qk[:, 1, :], onehot_in).then_inc(const_in, 16)
            with sp.Fori(0, IMAGES) as image:
                wait_apart(sp, y_sent, image * (16 * CT) + 16)
                sp.dma_start(x[:, :, :], x_in[image]).then_inc(x_in_sem, 16)
                for layer in range(LAYERS):
                    at = At(image, layer)
                    for c in range(CHUNKS):
                        if c == QK_CHUNKS + V_CHUNKS:
                            wait_apart(sp, score_ok, at.phases(HEADS * QT, HEADS * QT))
                        sp.wait_ge(w_hi_ok, at.phases(CHUNKS, c) + start(w_hi_ok))
                        sp.wait_ge(w_lo_ok, at.phases(CHUNKS, c) + start(w_lo_ok))
                        sp.dma_start(raw[:, :, :].rearrange("p a b -> p (a b)"),
                                     w_in[layer, c]).then_inc(raw_in, 16)
                        if c == QK_CHUNKS + V_CHUNKS - 1 and layer == 1:
                            sp.wait_ge(v_ok, at.phases(V_CHUNKS * QT, V_CHUNKS * QT))
                            sp.dma_start(stage[:, :], mask_in).then_inc(stage_in, 16)
                for o in range(CT):
                    wait_apart(sp, o_ok, At(image, 1).phases(2 * CT, 2 * o + 2))
                    sp.dma_start(y_out[image, :, o, :], x[:, o, :]).then_inc(y_sent, 16)
            sp.wait_ge(y_sent, 16 * CT * IMAGES + 16)

        @block.gpsimd
        def _(gp):
            for s, n in ((prob_ok, 2), (pv_done, P_SLOTS), (added, P_SLOTS), (head_done, 2),
                         (sum_mm, 2), (recip_ok, 1), (qk_ok, 4), (o_mm, 5), (w_hi_ok, 1), (w_lo_ok, 1),
                         (y_sent, 16)):
                gp.sem_inc(s, n)
            with gp.Fori(0, IMAGES) as image:
                for layer in range(LAYERS):
                    at = At(image, layer)
                    gp.wait_ge(var_ok, at.phases(1, 1))
                    nc.gpsimd.tensor_tensor(rstd[:, :], variance[:, :], power[:, :],
                                            ALU.pow).then_inc(rstd_ok, 1)
                    wait_apart(gp, v_ok, at.phases(V_CHUNKS * QT, V_CHUNKS * QT))
                    nc.gpsimd.memset(max_cols[:, :].bitcast(F32), 0.0).then_inc(cols_zero, 1)
                    def main(h, nxt, first):
                        total = acc[h.slot]
                        wait_apart(gp, sum_mm, h.heads(1, -1) + start(sum_mm))
                        if layer == 1:
                            nc.gpsimd.memset(total[:, :], 0.0).then_inc(acc_zero, 1)
                            gp.wait_ge(acc_zero, image * HEADS + (h.pair * 2 + (h.slot + 1)))
                        for t in range(QT):
                            a, b = query_span(layer, ORDER[layer][t])
                            if layer == 0 and t == 0:
                                continue
                            gp.wait_ge(prob_ok, h.heads(QT, t + 1) + start(prob_ok))
                            if t > 1 or (layer == 1 and t > 0):
                                gp.wait_ge(added, h.heads(QT, t) + start(added))
                            before = prob[:, 0, :] if layer == 0 and t == 1 else total[:, a:b]
                            nc.gpsimd.tensor_tensor(
                                total[:, a:b], before, prob[:, t % P_SLOTS, 0:b - a],
                                ALU.add).then_inc(added, 2 if layer == 0 and t == 1 else 1)

                    each_head(gp, image, layer, lambda h: None, main)

        @block.scalar
        def _(act):
            def weight_hi(at, c):
                act.wait_ge(raw_in, at.phases(16 * CHUNKS, 16 * (c + 1)))
                wait_multiplied(act, at, c - 2)
                nc.scalar.activation(w_hi[c % 2][:, :, :], raw[:, :, :], ACT.Copy).then_inc(w_hi_ok, 1)

            with act.Fori(0, IMAGES) as image:
                for layer in range(LAYERS):
                    at = At(image, layer)
                    weight_hi(at, 0)
                    for i in range(CT):
                        act.wait_ge(normed, at.phases(CT, i + 1))
                        nc.scalar.activation(a_hi[:, i, :], qk[:, i, :], ACT.Copy).then_inc(a_hi_ok, 1)
                    weight_hi(at, 1)
                    with act.Fori(0, QK_CHUNKS // 2) as i:
                        for s in range(2):
                            act.wait_ge(raw_in, i * 32 + at.phases(16 * CHUNKS, 16 * (s + 3)))
                            act.wait_ge(qk_mm, i * 8 + at.phases(4 * QK_CHUNKS, 4 * (s + 1)))
                            nc.scalar.activation(w_hi[s][:, :, :], raw[:, :, :],
                                                 ACT.Copy).then_inc(w_hi_ok, 1)
                    for c in range(V_CHUNKS):
                        for t in range(QT):
                            n = c * QT + t
                            act.wait_ge(v_mm, at.phases(V_CHUNKS * QT, n + 1))
                            nc.scalar.activation(v[:, t, c * CHUNK:(c + 1) * CHUNK],
                                                 score[:, n // 2 % 2, n % 2, 0:CHUNK],
                                                 ACT.Copy).then_inc(v_ok, 1)
                        if c == 0:
                            weight_hi(at, QK_CHUNKS + 2)

                    def prepare(h, step):
                        rows, where = head_rows(h.slot), pos_rows(h.slot)
                        if step == 0:
                            nc.scalar.activation(q_hi[h.slot][rows, :], qk[rows, h.pair, :],
                                                 ACT.Copy).then_inc(q_hi_ok, 1)
                        elif step == 4 and layer == 0:
                            nc.scalar.activation(q_rel[rows, :], qk[rows, h.pair, :],
                                                 ACT.Copy).then_inc(q_rel_ok, 1)
                        elif step == 5:
                            nc.scalar.activation(v_head[h.slot][:, :, :],
                                                 v[:, :, bass.ds(h.pair * 128 + h.slot * 64, HEAD_DIM)],
                                                 ACT.Copy).then_inc(v_head_ok, 1)
                        elif step == 1:
                            nc.scalar.activation(k_hi[h.slot][rows, :], qk[rows, h.pair + CT, :],
                                                 ACT.Copy).then_inc(k_hi_ok, 1)
                        elif step == 2:
                            nc.scalar.activation(q_max[h.slot][rows, :], qk[rows, h.pair, :],
                                                 ACT.Copy).then_inc(q_max_ok, 1)
                        elif step == 3 and layer == 0:
                            act.wait_ge(pos_mm, h.heads0(1, 1))
                            a = where.start
                            nc.scalar.activation(q_hi[h.slot][a:a + SIDE, :], small_all[a:a + SIDE, :],
                                                 ACT.Copy).then_inc(pos_hi_ok, 1)
                            nc.scalar.activation(
                                q_hi[h.slot][a + SIDE:a + 2 * SIDE, :].rearrange("p (h w) -> p w h", w=SIDE),
                                small_all[a + SIDE:a + 2 * SIDE, :].rearrange("p (w h) -> p w h", h=SIDE),
                                ACT.Copy).then_inc(pos_hi_ok, 1)

                    def sums_copy(h):
                        act.wait_ge(sum_mm, h.heads(1, 1) + start(sum_mm))
                        act.wait_ge(recip_ok, h.heads(1, 0) + start(recip_ok))
                        nc.scalar.activation(sums[:, :], small[:, 0, :], ACT.Copy).then_inc(sums_out, 1)

                    def main(h, nxt, first):
                        if nxt is not None:
                            prepare(nxt, 0)
                            prepare(nxt, 4)
                        r = max_row(h.slot)
                        act.wait_ge(max_row_mm, h.heads(1, 1))
                        nc.scalar.activation(q_max[h.slot][r:r + 1, HALF:], small[r:r + 1, 1, :],
                                             ACT.Copy).then_inc(max_row2_ok, 1)
                        for t in range(QT):
                            if nxt is not None and t == 2:
                                prepare(nxt, 3)
                            a, b = query_span(layer, ORDER[layer][t])
                            act.wait_ge(score_ok, h.heads(QT, t + 1))
                            act.wait_ge(pv_done, h.heads(QT, t + 1 - P_SLOTS) + start(pv_done))
                            act.wait_ge(added, h.heads(QT, t + 1 - P_SLOTS) + start(added))
                            nc.scalar.activation(
                                prob[:, t % P_SLOTS, 0:b - a],
                                score[:, t % 2, :, :].rearrange("p a b -> p (a b)")[:, 0:b - a],
                                ACT.Exp).then_inc(prob_ok, 1)
                            if not first and t == 0:
                                sums_copy(At(image, layer, h.pair if h.slot else h.pair - 1, 1 - h.slot))
                            if nxt is not None and t == 0:
                                prepare(nxt, 1)
                            if nxt is not None and t == 3:
                                act.wait_ge(pv_done, h.heads(QT, 0) + start(pv_done))
                                prepare(nxt, 5)
                                prepare(nxt, 2)
                        if nxt is None:
                            sums_copy(h)

                    def prepare_all(h):
                        act.wait_ge(w_lo_ok, at.phases(CHUNKS, QK_CHUNKS + V_CHUNKS) + start(w_lo_ok))
                        for step in (0, 4, 1, 2, 3, 5):
                            prepare(h, step)

                    each_head(act, image, layer, prepare_all, main)
                    for i in range(CT):
                        act.wait_ge(head_done, at.phases(HEADS, HEADS) + start(head_done))
                        if layer == 0:
                            nc.scalar.activation(a_hi[:, i, :], qk[:, i, :], ACT.Identity,
                                                 bias=bv[:, i:i + 1]).then_inc(o_hi_ok, 1)
                        else:
                            nc.scalar.activation(a_hi[:, i, :], qk[:, i, :], ACT.Copy).then_inc(o_hi_ok, 1)
                        if i in (0, 1):
                            weight_hi(at, QK_CHUNKS + V_CHUNKS + i)
                    weight_hi(at, CHUNKS - 1)

        @block.vector
        def _(dve):
            def weight_lo(at, c, more=0, s=None):
                dve.wait_ge(w_hi_ok, more + at.phases(CHUNKS, c + 1) + start(w_hi_ok))
                s = c % 2
                nc.vector.tensor_tensor(w_lo[s][:, :, :], raw[:, :, :], w_hi[s][:, :, :].bitcast(F32),
                                        ALU.subtract).then_inc(w_lo_ok, 1)

            nc.vector.memset(ones[:, :], 1.0).then_inc(const_ok, 1)
            nc.vector.memset(power[:, :], -0.5).then_inc(const_ok, 1)
            for s in range(2):
                nc.vector.memset(k_lo[s][pos_rows(s), :].bitcast(F32), 0.0).then_inc(const_ok, 1)
                nc.vector.memset(q_max[s][pos_rows(s), :].bitcast(F32), 0.0).then_inc(const_ok, 1)
            dve.wait_ge(const_ok, 6)
            for s in range(2):
                r = max_row(s)
                nc.vector.memset(k_lo[s][r:r + 1, :].bitcast(F32), -1.0).then_inc(const_ok, 1)
            dve.wait_ge(const_in, 16 * 8)
            nc.vector.tensor_copy(ident[:, :], qk[:, 0, 0:128]).then_inc(const_ok, 1)
            for s in range(2):
                nc.vector.tensor_copy(k_hi[s][pos_rows(s), :], qk[pos_rows(s), 1, :]).then_inc(const_ok, 1)
            dve.wait_ge(const_ok, N_SETUP)
            with dve.Fori(0, IMAGES) as image:
                for layer in range(LAYERS):
                    at = At(image, layer)
                    if layer == 0:
                        dve.wait_ge(x_in_sem, image * 16 + 16)
                    else:
                        dve.wait_ge(o_ok, at.phases(2 * CT, 0))
                    for i in range(CT):
                        for half in range(2):
                            nc.vector.bn_stats(bn[:, i, half, :], x[:, i, half * HALF:(half + 1) * HALF])\
                                .then_inc(bn_ok, 1)
                    wait_apart(dve, bn_ok, at.phases(2 * CT, 2 * CT))
                    for i in range(CT):
                        nc.vector.bn_aggr(mean_var[:, i, :], bn[:, i, :, :].rearrange("p a b -> p (a b)"))\
                            .then_inc(mv_ok, 1)
                    dve.wait_ge(gsum_ok, at.phases(1, 1))
                    nc.vector.tensor_copy(group_mv[:, :, :],
                                          small[:, 0, 0:2 * CT].rearrange("p (i k) -> p i k", k=2))\
                        .then_inc(gmv_ok, 1)
                    dve.wait_ge(gmv_ok, at.phases(1, 1))
                    dve.wait_ge(mv_ok, at.phases(CT, CT))
                    nc.vector.tensor_tensor(shift2[:, 0, :], mean_var[:, :, 0], group_mv[:, :, 0],
                                            ALU.subtract).then_inc(shift_ok, 1)
                    dve.wait_ge(shift_ok, at.phases(1, 1))
                    nc.vector.tensor_tensor(shift2[:, 1, :], shift2[:, 0, :], shift2[:, 0, :],
                                            ALU.mult).then_inc(shift2_ok, 1)
                    dve.wait_ge(gshift_ok, at.phases(1, 1))
                    nc.vector.scalar_tensor_tensor(variance[:, :], small[:, 1, 0:CT], EPS,
                                                   group_mv[:, :, 1], ALU.add, ALU.add).then_inc(var_ok, 1)
                    weight_lo(at, 0)
                    dve.wait_ge(rstd_ok, at.phases(1, 1))
                    for i in range(CT):
                        nc.vector.tensor_scalar(qk[:, i, :], x[:, i, :], group_mv[:, i, 0:1],
                                                rstd[:, i:i + 1], ALU.subtract, ALU.mult).then_inc(normed, 1)
                    for i in range(CT):
                        dve.wait_ge(a_hi_ok, at.phases(CT, i + 1))
                        nc.vector.tensor_tensor(a_lo[:, i, :], qk[:, i, :], a_hi[:, i, :].bitcast(F32),
                                                ALU.subtract).then_inc(a_lo_ok, 1)
                    weight_lo(at, 1)
                    with dve.Fori(0, QK_CHUNKS // 2) as i:
                        for s in range(2):
                            for k in range(4):
                                n, o = 4 * s + k, 2 * s + k // 2
                                dve.wait_ge(qk_mm, i * 8 + at.phases(4 * QK_CHUNKS, n + 1))
                                tile = i * 4 + o
                                dst = qk[:, tile, (k % 2) * HALF:(k % 2 + 1) * HALF]
                                src = score[:, n // 2 % 2, n % 2, :]
                                if layer == 0:
                                    nc.vector.tensor_scalar(dst, src, bqk[:, bass.ds(tile, 1)],
                                                            scale[:, bass.ds(tile, 1)],
                                                            ALU.add, ALU.mult).then_inc(qk_ok, 1)
                                else:
                                    nc.vector.tensor_scalar(dst, src, scale[:, bass.ds(tile, 1)], None,
                                                            ALU.mult).then_inc(qk_ok, 1)
                            weight_lo(at, s + 2, i * 2)
                    weight_lo(at, QK_CHUNKS + 2)
                    if layer == 1:
                        wait_apart(dve, stage_in, image * 16 + 16)
                        for s in range(2):
                            nc.vector.tensor_copy(q_hi[s][pos_rows(s), :], stage[pos_rows(s), :])\
                                .then_inc(mask_ok, 1)
                            nc.vector.memset(q_lo[s][pos_rows(s), :].bitcast(F32), 0.0)\
                                .then_inc(mask_ok, 1)

                    def prepare(h, part):
                        rows, where, s = head_rows(h.slot), pos_rows(h.slot), h.slot
                        if part == 0:
                            dve.wait_ge(q_hi_ok, h.heads(1, 1))
                            nc.vector.tensor_tensor(q_lo[s][rows, :], qk[rows, h.pair, :],
                                                    q_hi[s][rows, :].bitcast(F32),
                                                    ALU.subtract).then_inc(q_lo_ok, 1)
                        if part == 1:
                            dve.wait_ge(k_hi_ok, h.heads(1, 1))
                            nc.vector.tensor_tensor(k_lo[s][rows, :], qk[rows, h.pair + CT, :],
                                                    k_hi[s][rows, :].bitcast(F32),
                                                    ALU.subtract).then_inc(k_lo_ok, 1)
                        if part == 2 and layer == 0:
                            a = where.start
                            dve.wait_ge(pos_hi_ok, h.heads0(2, 1))
                            nc.vector.tensor_tensor(q_lo[s][a:a + SIDE, :], small_all[a:a + SIDE, :],
                                                    q_hi[s][a:a + SIDE, :].bitcast(F32),
                                                    ALU.subtract).then_inc(pos_lo_ok, 1)
                            dve.wait_ge(pos_hi_ok, h.heads0(2, 2))
                            a += SIDE
                            nc.vector.tensor_tensor(
                                q_lo[s][a:a + SIDE, :].rearrange("p (h w) -> p w h", w=SIDE),
                                small_all[a:a + SIDE, :].rearrange("p (w h) -> p w h", h=SIDE),
                                q_hi[s][a:a + SIDE, :].rearrange("p (h w) -> p w h", w=SIDE).bitcast(F32),
                                ALU.subtract).then_inc(pos_lo_ok, 1)

                    def maxima(h):
                        for n in range(MAX_PER[layer]):
                            t = n // 2 if layer == 0 else n
                            size = HALF if layer == 0 else key_span(t)[1] - key_span(t)[0]
                            dve.wait_ge(max_mm, h.heads2(*MAX_PER, n + 1))
                            nc.vector.reduce_max(max_part[:, n:n + 1], small[:, n % 2, 0:size],
                                                 AX.X).then_inc(max_part_ok, 1)
                        dve.wait_ge(max_part_ok, h.heads2(*MAX_PER, MAX_PER[layer]))
                        dst = max_cols[:, 64:].rearrange("p (t c) -> p t c", c=128)[:, :, 0]
                        if layer == 0:
                            both = max_part[:, :].rearrange("p (t k) -> p t k", k=2)
                            nc.vector.tensor_tensor(dst, both[:, :, 0], both[:, :, 1],
                                                    ALU.max).then_inc(max_cols_ok, 1)
                        else:
                            nc.vector.tensor_copy(dst, max_part[:, 0:QT]).then_inc(max_cols_ok, 1)

                    def invert(h):
                        dve.wait_ge(sums_out, h.heads(1, 1))
                        dve.wait_ge(head_done, h.heads(1, 0) + start(head_done))
                        nc.vector.reciprocal(recip[:, :], sums[:, :]).then_inc(recip_ok, 1)

                    def normalise(h):
                        dve.wait_ge(recip_ok, h.heads(1, 1) + start(recip_ok))
                        rows = head_rows(h.slot)
                        for half in range(2):
                            part = head_rows(half)
                            last = nc.vector.tensor_tensor(
                                qk[rows, h.pair, half * HALF:(half + 1) * HALF],
                                head_out[part, h.slot, :], recip[part, :], ALU.mult)
                            last.then_inc(*((head_done, 1) if half else (recip_used, 1)))

                    def prepare_all(h):
                        dve.wait_ge(cols_zero, at.phases(1, 1))
                        prepare(h, 0)
                        prepare(h, 1)
                        prepare(h, 2)
                        maxima(h)

                    def main(h, nxt, first):
                        r = max_row(h.slot)
                        before = At(image, layer, h.pair if h.slot else h.pair - 1, 1 - h.slot)
                        dve.wait_ge(max_row_mm, h.heads(1, 1))
                        nc.vector.tensor_copy(q_max[h.slot][r:r + 1, 0:HALF], small[r:r + 1, 0, :])\
                            .then_inc(max_row_ok, 1)
                        if nxt is not None:
                            prepare(nxt, 0)
                        if not first:
                            invert(before)
                        if nxt is not None:
                            prepare(nxt, 1)
                            prepare(nxt, 2)
                        if not first:
                            normalise(before)
                        if nxt is not None:
                            maxima(nxt)
                        else:
                            invert(h)
                            normalise(h)

                    each_head(dve, image, layer, prepare_all, main)
                    for i in range(CT):
                        dve.wait_ge(o_hi_ok, at.phases(CT, i + 1))
                        if layer == 0:
                            nc.vector.scalar_tensor_tensor(a_lo[:, i, :], qk[:, i, :], bv[:, i:i + 1],
                                                           a_hi[:, i, :].bitcast(F32), ALU.add,
                                                           ALU.subtract).then_inc(o_lo_ok, 1)
                        else:
                            nc.vector.tensor_tensor(a_lo[:, i, :], qk[:, i, :], a_hi[:, i, :].bitcast(F32),
                                                    ALU.subtract).then_inc(o_lo_ok, 1)
                        if i in (0, 1):
                            weight_lo(at, QK_CHUNKS + V_CHUNKS + i)
                    for n in range(2 * CT):
                        o, half = n // 2, n % 2
                        dve.wait_ge(o_mm, at.phases(2 * CT, n + 1) + start(o_mm))
                        dst = x[:, o, half * HALF:(half + 1) * HALF]
                        src = score[:, n // 2 % 2, n % 2, :]
                        if layer == 0:
                            nc.vector.scalar_tensor_tensor(dst, src, bp[:, o:o + 1], dst, ALU.add,
                                                           ALU.add).then_inc(o_ok, 1)
                        else:
                            nc.vector.tensor_tensor(dst, src, dst, ALU.add).then_inc(o_ok, 1)
                        if n == 3:
                            weight_lo(at, CHUNKS - 1)

        @block.tensor
        def _(pe):
            def split_product(out, w, a, first, last):
                nc.tensor.matmul(out, w[0], a[0], start=first, stop=False)
                nc.tensor.matmul(out, w[0], a[1], start=False, stop=False)
                return nc.tensor.matmul(out, w[1], a[0], start=False, stop=last)

            pe.wait_ge(const_ok, N_SETUP)
            with pe.Fori(0, IMAGES) as image:
                for layer in range(LAYERS):
                    at = At(image, layer)
                    pe.wait_ge(mv_ok, at.phases(CT, CT))

                    def averages(bank, stats, width, done):
                        for j in range(CT):
                            from_tiles = [(n, i + j // GROUP_SPAN * GROUP_SPAN)
                                          for n, (i, k) in enumerate(blocks) if k == j % GROUP_SPAN]
                            for k, (n, i) in enumerate(from_tiles):
                                last = nc.tensor.matmul(small[:, bank, j * width:(j + 1) * width],
                                                        group[:, n, :], stats(i), start=(k == 0),
                                                        stop=(k == len(from_tiles) - 1))
                        last.then_inc(done, 1)

                    averages(0, lambda i: mean_var[:, i, :], 2, gsum_ok)
                    pe.wait_ge(shift2_ok, at.phases(1, 1))
                    averages(1, lambda i: shift2[:, 1, i:i + 1], 1, gshift_ok)
                    wait_apart(pe, a_lo_ok, at.phases(CT, CT))
                    with pe.Fori(0, QK_CHUNKS // 2) as i:
                        for s in range(2):
                            pe.wait_ge(w_hi_ok, i * 2 + at.phases(CHUNKS, s + 1) + start(w_hi_ok))
                            pe.wait_ge(w_lo_ok, i * 2 + at.phases(CHUNKS, s + 1) + start(w_lo_ok))
                            for k in range(4):
                                n, cols = 4 * s + k, slice(k // 2 * 128, k // 2 * 128 + 128)
                                half = slice(k % 2 * HALF, (k % 2 + 1) * HALF)
                                pe.wait_ge(qk_ok, i * 8 + at.phases(4 * QK_CHUNKS, n - 3) + start(qk_ok))
                                for c in range(CT):
                                    last = split_product(score[:, n // 2 % 2, n % 2, :],
                                                         (w_hi[s][:, c, cols], w_lo[s][:, c, cols]),
                                                         (a_hi[:, c, half], a_lo[:, c, half]),
                                                         c == 0, c == CT - 1)
                                last.then_inc(qk_mm, 1)
                    for c in range(V_CHUNKS):
                        chunk, s = QK_CHUNKS + c, c % 2
                        pe.wait_ge(w_lo_ok, at.phases(CHUNKS, chunk + 1) + start(w_lo_ok))
                        for t in range(QT):
                            n = c * QT + t
                            if n < 4:
                                pe.wait_ge(qk_ok, at.phases(4 * QK_CHUNKS, 4 * QK_CHUNKS - 3 + n) + start(qk_ok))
                            else:
                                pe.wait_ge(v_ok, at.phases(V_CHUNKS * QT, n - 3))
                            tok = slice(t * 128, (t + 1) * 128)
                            for i in range(CT):
                                last = split_product(score[:, n // 2 % 2, n % 2, 0:CHUNK],
                                                     (a_hi[:, i, tok], a_lo[:, i, tok]),
                                                     (w_hi[s][:, i, :], w_lo[s][:, i, :]),
                                                     i == 0, i == CT - 1)
                            last.then_inc(v_mm, 1)

                    def position(h):
                        rows, a = head_rows(h.slot), pos_rows(h.slot).start
                        wait_apart(pe, q_rel_ok, h.heads0(1, 1))
                        by_row = q_rel[rows, :].rearrange("p (h w) -> p h w", w=SIDE)
                        for i in range(SIDE):
                            window = slice(SIDE - 1 - i, 2 * SIDE - 1 - i)
                            nc.tensor.matmul(small_all[a:a + SIDE, i * SIDE:(i + 1) * SIDE],
                                             rel[rows, 0, window], by_row[:, i, :], start=True, stop=True)
                            last = nc.tensor.matmul(small_all[a + SIDE:a + 2 * SIDE, i * SIDE:(i + 1) * SIDE],
                                                    rel[rows, 1, window], by_row[:, :, i],
                                                    start=True, stop=True)
                        last.then_inc(pos_mm, 1)

                    def maximum(h, n):
                        s, t = h.slot, (n // 2 if layer == 0 else n)
                        a, b = (n % 2 * HALF, (n % 2 + 1) * HALF) if layer == 0 else key_span(t)
                        if n == 0:
                            pe.wait_ge(q_hi_ok, h.heads(1, 1))
                            pe.wait_ge(k_hi_ok, h.heads(1, 1))
                            if layer == 0:
                                pe.wait_ge(pos_lo_ok, h.heads0(2, 2))
                        if n >= 2:
                            pe.wait_ge(max_part_ok, h.heads2(*MAX_PER, n - 1))
                        nc.tensor.matmul(small[:, n % 2, 0:b - a], q_hi[s][:, t * 128:(t + 1) * 128],
                                         k_hi[s][:, a:b], start=True, stop=True).then_inc(max_mm, 1)

                    def maximum_row(h):
                        pe.wait_ge(max_cols_ok, h.heads(1, 1))
                        for t in range(QT):
                            a = t * 128 + 64 * h.slot
                            last = nc.tensor.matmul(small_all[:, t * 128:(t + 1) * 128],
                                                    max_cols[:, a:a + 128], ident[:, :],
                                                    start=True, stop=True)
                        last.then_inc(max_row_mm, 1)

                    def scores(h, step, part):
                        s, t = h.slot, ORDER[layer][step]
                        a, b = query_span(layer, t)
                        keys = slice(t * 128, (t + 1) * 128)
                        pieces = [(a, a + HALF), (a + HALF, b)] if b - a > HALF else [(a, b)]
                        if part == 0:
                            pe.wait_ge(prob_ok, h.heads(QT, step - 1) + start(prob_ok))
                            if step == 0:
                                pe.wait_ge(q_lo_ok, h.heads(1, 1))
                        elif step == 0:
                            pe.wait_ge(k_lo_ok, h.heads(1, 1))
                            pe.wait_ge(q_max_ok, h.heads(1, 1))
                            pe.wait_ge(max_row_ok, h.heads(1, 1))
                            pe.wait_ge(max_row2_ok, h.heads(1, 1))
                        for w, x_ in (((k_lo, q_max),) if part else ((k_hi, q_hi), (k_hi, q_lo))):
                            for n, (p, q) in enumerate(pieces):
                                last = nc.tensor.matmul(score[:, step % 2, n, 0:q - p], w[s][:, keys],
                                                        x_[s][:, p:q], start=(x_ is q_hi), stop=(part == 1))
                        if part == 1:
                            last.then_inc(score_ok, 1)

                    def values(h, step):
                        s = h.slot
                        steps = [step] if layer == 0 else [step - 1, step]
                        if step == 0 or (layer == 1 and step == 1):
                            pe.wait_ge(v_head_ok, h.heads(1, 1))
                            pe.wait_ge(head_done, h.heads(1, -1) + start(head_done))
                        pe.wait_ge(prob_ok, h.heads(QT, step + 1) + start(prob_ok))
                        for u in steps:
                            t = ORDER[layer][u]
                            a, b = query_span(layer, t)
                            for half in range(2):
                                p, q = max(a, half * HALF), min(b, (half + 1) * HALF)
                                if p >= q:
                                    continue
                                first = (u == 0 or (layer == 1 and u == 1))
                                last_u = QT - 1 if layer == 0 else QT - 1
                                out = head_out[head_rows(half), s, p - half * HALF:q - half * HALF]
                                last = nc.tensor.matmul(out, v_head[s][:, t, :],
                                                        prob[:, u % P_SLOTS, p - a:q - a],
                                                        start=first, stop=(u == last_u),
                                                        skip_group_check=(layer == 1))
                        last.then_inc(pv_done, len(steps))

                    def sums(h):
                        pe.wait_ge(added, h.heads(QT, QT) + start(added))
                        for half in range(2):
                            last = nc.tensor.matmul(small[head_rows(half), 0, :], ones[:, :],
                                                    acc[h.slot][:, half * HALF:(half + 1) * HALF],
                                                    start=True, stop=True)
                        last.then_inc(sum_mm, 1)

                    def prepare(h):
                        pe.wait_ge(v_ok, at.phases(V_CHUNKS * QT, V_CHUNKS * QT))
                        if layer == 0:
                            position(h)
                        else:
                            pe.wait_ge(mask_ok, image * 4 + 4)
                        for n in range(MAX_PER[layer]):
                            maximum(h, n)

                    def main(h, nxt, first):
                        before = None
                        if not first:
                            before = At(image, layer, h.pair if h.slot else h.pair - 1, 1 - h.slot)

                        def maxima(t, part):
                            if nxt is not None:
                                for n in max_turn(layer, t, part):
                                    maximum(nxt, n)

                        for t in range(QT):
                            scores(h, t, 0)
                            if t == 0:
                                maximum_row(h)
                                if before is not None:
                                    values(before, QT - 1)
                            maxima(t, 0)
                            scores(h, t, 1)
                            maxima(t, 1)
                            if t > 0 and (layer == 0 or t % 2 == 0):
                                values(h, t - 1)
                            maxima(t, 2)
                            if t == 0 and before is not None:
                                sums(before)
                            if t == 1:
                                if before is not None:
                                    pe.wait_ge(sums_out, before.heads(1, 1))
                                if nxt is not None and layer == 0:
                                    position(nxt)
                        if nxt is None:
                            values(h, QT - 1)
                            sums(h)

                    each_head(pe, image, layer, prepare, main)
                    for n in range(2 * CT):
                        o, half = n // 2, n % 2
                        chunk = QK_CHUNKS + V_CHUNKS + o // 2
                        s, cols = chunk % 2, slice(o % 2 * 128, o % 2 * 128 + 128)
                        if n % 4 == 0:
                            pe.wait_ge(w_lo_ok, at.phases(CHUNKS, chunk + 1) + start(w_lo_ok))
                        if n >= 4:
                            pe.wait_ge(o_ok, at.phases(2 * CT, n - 3))
                        h = slice(half * HALF, (half + 1) * HALF)
                        for c in range(CT):
                            if n == 0:
                                pe.wait_ge(o_lo_ok, at.phases(CT, c + 1))
                            last = split_product(score[:, n // 2 % 2, n % 2, :],
                                                 (w_hi[s][:, c, cols], w_lo[s][:, c, cols]),
                                                 (a_hi[:, c, h], a_lo[:, c, h]), c == 0, c == CT - 1)
                        last.then_inc(o_mm, 1)
    

def kernel(**inputs):
    import numpy as np
    import concourse.bacc as bacc
    from concourse.bass_utils import run_bass_kernel_spmd

    f32 = np.float32

    def tiles(a):
        a = np.asarray(a)
        return np.ascontiguousarray(a.reshape(CT, 128, -1).transpose(1, 0, 2))

    def vector_tiles(a):
        return np.ascontiguousarray(np.asarray(a).reshape(-1, 128).T)

    def chunks(w):
        w = tiles(w)
        return [w[:, :, n:n + CHUNK].reshape(128, CT * CHUNK) for n in range(0, w.shape[2], CHUNK)]

    x = np.asarray(inputs["x"])
    x_t = x.reshape(IMAGES, TOKENS, CT, 128).transpose(0, 3, 2, 1)
    qkv = np.asarray(inputs["L1_conv_qkv_w"])
    weights = np.stack([
        np.stack(sum((chunks(inputs[f"L0_conv_W{n}"]) for n in "qkvp"), [])),
        np.stack(chunks(qkv.T) + chunks(np.asarray(inputs["L1_conv_out_w"]).T)),
    ])
    rel = np.stack([np.asarray(inputs[f"L0_conv_rel_{n}"])[::-1].T for n in "hw"], axis=1)
    token = np.arange(TOKENS)
    line = np.arange(SIDE)
    onehot = np.concatenate([token // SIDE == line[:, None], token % SIDE == line[:, None]]).astype(f32)
    near = np.clip(line, RADIUS, SIDE - 1 - RADIUS)
    far = np.abs(near[None, :] - line[:, None]) > RADIUS
    mask = np.where(np.concatenate([far[:, token // SIDE], far[:, token % SIDE]]), f32(-2.0 ** 100), f32(0))
    channel = np.arange(GROUP_SPAN * 128)
    same = (channel[:, None] // GROUP == channel[None, :] // GROUP) * (1.0 / GROUP)
    group = np.stack([same[i * 128:(i + 1) * 128, j * 128:(j + 1) * 128] for i, j in group_blocks()], axis=1)
    scale = np.ones((128, QK_TILES), f32)
    scale[:, CT:] = HEAD_DIM ** -0.5
    arrays = {
        "x_t": x_t,
        "weights": weights,
        "bias_qk": np.concatenate([vector_tiles(inputs[f"L0_conv_b{n}"]) for n in "qk"], axis=1),
        "scale_qk": scale,
        "bias_v": vector_tiles(inputs["L0_conv_bv"]),
        "bias_out": vector_tiles(inputs["L0_conv_bp"]),
        "rel": np.concatenate([rel, rel]),
        "onehot": np.concatenate([onehot, onehot]),
        "mask": np.concatenate([mask, mask]).astype(f32),
        "group": group.astype(f32),
        "ident": np.eye(128, dtype=f32),
    }
    arrays = {k: np.ascontiguousarray(a) for k, a in arrays.items()}
    nc = bacc.Bacc("TRN2", target_bir_lowering=False, num_devices=1)
    args = [nc.dram_tensor(k, a.shape, mybir.dt.from_np(a.dtype), kind="ExternalInput").ap()
            for k, a in arrays.items()]
    y = nc.dram_tensor("y_t", (IMAGES, 128, CT, TOKENS), F32, kind="ExternalOutput").ap()
    build(nc, *args, y)
    r = run_bass_kernel_spmd(nc, [arrays], core_ids=[0])
    y_t = np.asarray(r.results[0]["y_t"])
    return np.ascontiguousarray(y_t.transpose(0, 3, 2, 1)).reshape(x.shape)
```

```python
import concourse.bass as bass
from concourse import mybir

F32 = mybir.dt.float32
F32R = mybir.dt.float32r
ALU = mybir.AluOpType
ACT = mybir.ActivationFunctionType
AX = mybir.AxisListType

IMAGES, SIDE, CHANNELS, HEADS, LAYERS = 4, 32, 768, 12, 2
TOKENS = SIDE * SIDE
HEAD_DIM = CHANNELS // HEADS
CT = CHANNELS // 128
QT = TOKENS // 128
HALF = TOKENS // 2
CHUNK = 256
QK_CHUNKS, V_CHUNKS, O_CHUNKS = 6, 3, 3
CHUNKS = QK_CHUNKS + V_CHUNKS + O_CHUNKS
QK_TILES = 2 * CT
REL = 2 * SIDE - 1
GROUP = CHANNELS // 32
GROUP_SPAN = 3
EPS = 1e-5
REACH, RADIUS = 7, 3
P_SLOTS = 4
ORDER = [[0, 1, 2, 3, 4, 5, 6, 7], [0, 7, 1, 6, 2, 5, 3, 4]]


def centre(i):
    return min(max(i, RADIUS), SIDE - 1 - RADIUS)


def query_span(layer, key_tile):
    if layer == 0:
        return 0, TOKENS
    rows = range(4 * key_tile, 4 * key_tile + 4)
    near = [i for i in range(SIDE) if any(abs(centre(i) - r) <= RADIUS for r in rows)]
    return near[0] * SIDE, (near[-1] + 1) * SIDE


def key_span(query_tile):
    c = [centre(i) for i in range(4 * query_tile, 4 * query_tile + 4)]
    return (min(c) - RADIUS) * SIDE, (max(c) + RADIUS + 1) * SIDE


def group_blocks():
    return [(i, j) for j in range(GROUP_SPAN) for i in range(GROUP_SPAN) if abs(i - j) <= 1]


class Memory:

    def __init__(self, nc, at):
        self.nc, self.at = nc, at

    def put(self, name, shape, dtype=F32):
        size = 4
        for n in shape[1:]:
            size *= n
        t = self.nc.alloc_sbuf_tensor_at(name, shape, dtype, offset=self.at)
        self.at += (size + 31) // 32 * 32
        return t


def build(nc, x_in, w_in, bqk_in, scale_in, bv_in, bp_in, rel_in, onehot_in, mask_in, group_in,
          ident_in, y_out):
    blocks = group_blocks()
    m = Memory(nc, (nc.sbuf_base + 31) // 32 * 32)
    x = m.put("x", [128, CT, TOKENS])
    qk = m.put("qk", [128, QK_TILES, TOKENS])
    v = m.put("v", [128, QT, CHANNELS])
    k_hi = [m.put(f"k_hi{s}", [128, TOKENS], F32R) for s in range(2)]
    k_lo = [m.put(f"k_lo{s}", [128, TOKENS], F32R) for s in range(2)]
    q_max = [m.put(f"q_max{s}", [128, TOKENS], F32R) for s in range(2)]
    w_hi0 = m.put("w_hi0", [128, CT, CHUNK], F32R)
    w_lo0 = m.put("w_lo0", [128, CT, CHUNK], F32R)
    group = m.put("group", [128, len(blocks), 128])
    ident = m.put("ident", [128, 128], F32R)
    ones = m.put("ones", [128, 64])
    rel = m.put("rel", [128, 2, REL])
    bqk = m.put("bqk", [128, QK_TILES])
    scale = m.put("scale", [128, QK_TILES])
    bv = m.put("bv", [128, CT])
    bp = m.put("bp", [128, CT])
    bn = m.put("bn", [128, CT, 2, 6])
    mean_var = m.put("mean_var", [128, CT, 2])
    group_mv = m.put("group_mv", [128, CT, 2])
    shift2 = m.put("shift2", [128, 2, CT])
    variance = m.put("variance", [128, CT])
    power = m.put("power", [128, CT])
    rstd = m.put("rstd", [128, CT])
    max_part = m.put("max_part", [128, 2 * QT])
    shared = m.at
    q_hi = [m.put(f"q_hi{s}", [128, TOKENS], F32R) for s in range(2)]
    q_lo = [m.put(f"q_lo{s}", [128, TOKENS], F32R) for s in range(2)]
    end = m.at
    m.at = shared
    w_hi1 = m.put("w_hi1", [128, CT, CHUNK], F32R)
    w_lo1 = m.put("w_lo1", [128, CT, CHUNK], F32R)
    raw = m.put("raw", [128, CT, CHUNK])
    m.at -= TOKENS * 4
    stage = m.put("stage", [128, TOKENS])
    m.at = max(m.at, end)
    w_hi, w_lo = [w_hi0, w_hi1], [w_lo0, w_lo1]
    shared = m.at
    a_hi = m.put("a_hi", [128, CT, TOKENS], F32R)
    a_lo = m.put("a_lo", [128, CT, TOKENS], F32R)
    assert m.at <= nc.sbuf_usable_end
    m.at = shared
    prob = m.put("prob", [128, P_SLOTS, TOKENS])
    acc = [m.put(f"acc{s}", [128, TOKENS]) for s in range(2)]
    v_head = [m.put(f"v_head{s}", [128, QT, HEAD_DIM]) for s in range(2)]
    q_rel = m.put("q_rel", [128, TOKENS])
    max_cols = m.put("max_cols", [128, 64 + QT * 128], F32R)
    m.at = shared + (2 * CT - 1) * TOKENS * 4
    sums = m.put("sums", [128, HALF])
    recip = m.put("recip", [128, HALF])

    score = nc.alloc_psum_tensor("score", [128, 2, 2, HALF], F32)
    small = nc.alloc_psum_tensor("small", [128, 2, HALF], F32)
    head_out = nc.alloc_psum_tensor("head_out", [128, 2, HALF], F32)
    small_all = small[:, :, :].rearrange("p a b -> p (a b)")

    def sem(name):
        return nc.alloc_semaphore(name)

    const_in, const_ok, stage_in, next_in = (sem(n) for n in ("const_in", "const_ok", "stage_in", "next_in"))
    x_in_sem, raw_in, y_sent = sem("x_in"), sem("raw_in"), sem("y_sent")
    bn_ok, mv_ok, gsum_ok, gmv_ok, shift_ok, shift2_ok = (sem(n) for n in (
        "bn_ok", "mv_ok", "gsum_ok", "gmv_ok", "shift_ok", "shift2_ok"))
    gshift_ok, var_ok, rstd_ok, normed = (sem(n) for n in ("gshift_ok", "var_ok", "rstd_ok", "normed"))
    a_hi_ok, a_lo_ok, w_hi_ok, w_lo_ok = (sem(n) for n in ("a_hi_ok", "a_lo_ok", "w_hi_ok", "w_lo_ok"))
    qk_mm, qk_ok, v_mm, v_ok, o_mm, o_ok = (sem(n) for n in (
        "qk_mm", "qk_ok", "v_mm", "v_ok", "o_mm", "o_ok"))
    mask_ok, cols_zero, o_hi_ok, o_lo_ok = (sem(n) for n in ("mask_ok", "cols_zero", "o_hi_ok", "o_lo_ok"))
    q_rel_ok, v_head_ok, q_hi_ok, k_hi_ok, q_max_ok, q_lo_ok, k_lo_ok = (sem(n) for n in (
        "q_rel_ok", "v_head_ok", "q_hi_ok", "k_hi_ok", "q_max_ok", "q_lo_ok", "k_lo_ok"))
    pos_mm, pos_hi_ok, pos_lo_ok = sem("pos_mm"), sem("pos_hi_ok"), sem("pos_lo_ok")
    max_mm, max_part_ok, max_cols_ok, max_row_mm, max_row_ok = (sem(n) for n in (
        "max_mm", "max_part_ok", "max_cols_ok", "max_row_mm", "max_row_ok"))
    max_row2_ok, sums_out = sem("max_row2_ok"), sem("sums_out")
    score_ok, prob_ok, pv_done, added, sum_mm, recip_ok, head_done = (sem(n) for n in (
        "score_ok", "prob_ok", "pv_done", "added", "sum_mm", "recip_ok", "head_done"))
    acc_zero, recip_used = sem("acc_zero"), sem("recip_used")
    passed = {e.engine: sem(f"passed_{n}") for n, e in (
        ("tensor", nc.tensor), ("vector", nc.vector), ("gpsimd", nc.gpsimd), ("sync", nc.sync))}

    START = {id(prob_ok): 2, id(pv_done): P_SLOTS, id(added): P_SLOTS, id(head_done): 2,
             id(sum_mm): 2, id(recip_ok): 1, id(qk_ok): 4, id(o_mm): 5, id(w_hi_ok): 1, id(w_lo_ok): 1}

    def start(s):
        return START.get(id(s), 0)

    def head_rows(s):
        return slice(64 * s, 64 * s + 64)

    def pos_rows(s):
        return slice(64 - 64 * s, 128 - 64 * s)

    def max_row(s):
        return 64 - 64 * s

    class At:

        def __init__(self, image, layer, pair=None, slot=None):
            self.image, self.layer, self.pair, self.slot = image, layer, pair, slot

        def after(self):
            return At(self.image, 1) if self.layer == 0 else At(self.image + 1, 0)

        def phases(self, per, extra):
            return self.image * (2 * per) + (self.layer * per + extra)

        def layer0(self, per, extra):
            return self.image * per + extra

        def heads(self, per, extra):
            return self.image * (2 * HEADS * per) + self.pair * (2 * per) + (
                (self.layer * HEADS + self.slot) * per + extra)

        def heads2(self, per0, per1, extra):
            per = per1 if self.layer else per0
            return self.image * (HEADS * (per0 + per1)) + self.pair * (2 * per) + (
                self.layer * HEADS * per0 + self.slot * per + extra)

        def heads0(self, per, extra):
            return self.image * (HEADS * per) + self.pair * (2 * per) + (self.slot * per + extra)

    def each_head(engine, image, layer, prepare, main):
        prepare(At(image, layer, 0, 0))
        main(At(image, layer, 0, 0), At(image, layer, 0, 1), True)
        with engine.Fori(0, HEADS // 2 - 1) as j:
            main(At(image, layer, j, 1), At(image, layer, j + 1, 0), False)
            main(At(image, layer, j + 1, 0), At(image, layer, j + 1, 1), False)
        main(At(image, layer, HEADS // 2 - 1, 1), None, False)

    N_SETUP = 11
    NORM_AT = CT - 1

    def wait_apart(engine, semaphore, count):
        engine.wait_ge(semaphore, count)
        engine.sem_inc(passed[engine.engine], 1)

    def wait_multiplied(engine, at, c):
        if c < QK_CHUNKS and c >= 0:
            engine.wait_ge(qk_mm, at.phases(4 * QK_CHUNKS, 4 * (c + 1)))
        elif c >= QK_CHUNKS and c < QK_CHUNKS + V_CHUNKS:
            engine.wait_ge(v_mm, at.phases(V_CHUNKS * QT, QT * (c - QK_CHUNKS + 1)))
        else:
            engine.wait_ge(o_mm, at.phases(2 * CT, 4 * (c % CHUNKS - (CHUNKS - O_CHUNKS) + 1)
                                           - (2 * CT if c < 0 else 0)) + start(o_mm))

    MAX_IN_STEP = [[0, 0, 0, 2, 3, 3, 4, 4], [0, 0, 0, 0, 1, 2, 2, 3]]
    MAX_AFTER = {0: [], 1: [2], 2: [0, 2], 3: [0, 1, 2], 4: [0, 1, 2, 2]}

    def max_turn(layer, t, part):
        n = sum(MAX_IN_STEP[layer][:t])
        after = [1, 2] if t == 3 and layer == 0 else MAX_AFTER[MAX_IN_STEP[layer][t]]
        return [n + k for k, p in enumerate(after) if p == part]

    MAX_EVERY = [2, 3]
    MAX_PER = [2 * QT, QT]

    with nc.Block() as block:

        @block.sync
        def _(sp):
            for dst, src in ((group, group_in), (rel, rel_in), (bqk, bqk_in), (scale, scale_in),
                             (bv, bv_in), (bp, bp_in)):
                sp.dma_start(dst[:], src).then_inc(const_in, 16)
            sp.dma_start(qk[:, 0, 0:128], ident_in).then_inc(const_in, 16)
            sp.dma_start(qk[:, 1, :], onehot_in).then_inc(const_in, 16)
            sp.dma_start(qk[:, CT:QK_TILES, :], x_in[0]).then_inc(next_in, 16)
            sp.dma_start(raw[:, :, :].rearrange("p a b -> p (a b)"), w_in[0, 0]).then_inc(raw_in, 16)
            with sp.Fori(0, IMAGES) as image:
                for layer in range(LAYERS):
                    at = At(image, layer)
                    for c in range(1, CHUNKS + 1):
                        if c == QK_CHUNKS + V_CHUNKS:
                            if layer == 1:
                                sp.wait_ge(w_hi_ok, at.phases(CHUNKS, c) + start(w_hi_ok))
                                sp.wait_ge(w_lo_ok, at.phases(CHUNKS, c) + start(w_lo_ok))
                                sp.dma_start(stage[:, :], mask_in).then_inc(stage_in, 16)
                            wait_apart(sp, score_ok, at.phases(HEADS * QT, HEADS * QT))
                        sp.wait_ge(w_hi_ok, at.phases(CHUNKS, c) + start(w_hi_ok))
                        sp.wait_ge(w_lo_ok, at.phases(CHUNKS, c) + start(w_lo_ok))
                        sp.dma_start(raw[:, :, :].rearrange("p a b -> p (a b)"),
                                     w_in[layer if c < CHUNKS else 1 - layer, c % CHUNKS])\
                            .then_inc(raw_in, 16)
                        if c == 2 and layer == 0:
                            wait_apart(sp, y_sent, image * (16 * CT) + 16)
                            sp.dma_start(x[:, :, :], x_in[image]).then_inc(x_in_sem, 16)
                        if c == QK_CHUNKS + V_CHUNKS and layer == 1:
                            sp.dma_start(qk[:, CT:QK_TILES, :], x_in[image + 1]).then_inc(next_in, 16)
                for o in range(CT):
                    wait_apart(sp, o_ok, At(image, 1).phases(2 * CT, 2 * o + 2))
                    sp.dma_start(y_out[image, :, o, :], x[:, o, :]).then_inc(y_sent, 16)
            sp.wait_ge(y_sent, 16 * CT * IMAGES + 16)

        @block.gpsimd
        def _(gp):
            for s, n in ((prob_ok, 2), (pv_done, P_SLOTS), (added, P_SLOTS), (head_done, 2),
                         (sum_mm, 2), (recip_ok, 1), (qk_ok, 4), (o_mm, 5), (w_hi_ok, 1), (w_lo_ok, 1),
                         (y_sent, 16)):
                gp.sem_inc(s, n)

            def deviation(at):
                gp.wait_ge(var_ok, at.phases(1, 1))
                nc.gpsimd.tensor_tensor(rstd[:, :], variance[:, :], power[:, :],
                                        ALU.pow).then_inc(rstd_ok, 1)

            deviation(At(0, 0))
            with gp.Fori(0, IMAGES) as image:
                for layer in range(LAYERS):
                    at = At(image, layer)
                    wait_apart(gp, v_ok, at.phases(V_CHUNKS * QT, V_CHUNKS * QT))
                    nc.gpsimd.memset(max_cols[:, :].bitcast(F32), 0.0).then_inc(cols_zero, 1)
                    def main(h, nxt, first):
                        total = acc[h.slot]
                        wait_apart(gp, sum_mm, h.heads(1, -1) + start(sum_mm))
                        if layer == 1:
                            nc.gpsimd.memset(total[:, :], 0.0).then_inc(acc_zero, 1)
                            gp.wait_ge(acc_zero, image * HEADS + (h.pair * 2 + (h.slot + 1)))
                        for t in range(QT):
                            a, b = query_span(layer, ORDER[layer][t])
                            if layer == 0 and t == 0:
                                continue
                            gp.wait_ge(prob_ok, h.heads(QT, t + 1) + start(prob_ok))
                            if t > 1 or (layer == 1 and t > 0):
                                gp.wait_ge(added, h.heads(QT, t) + start(added))
                            before = prob[:, 0, :] if layer == 0 and t == 1 else total[:, a:b]
                            nc.gpsimd.tensor_tensor(
                                total[:, a:b], before, prob[:, t % P_SLOTS, 0:b - a],
                                ALU.add).then_inc(added, 2 if layer == 0 and t == 1 else 1)

                    each_head(gp, image, layer, lambda h: None, main)
                    deviation(at.after())

        @block.scalar
        def _(act):
            def weight_hi(at, c):
                act.wait_ge(raw_in, at.phases(16 * CHUNKS, 16 * (c + 1)))
                wait_multiplied(act, at, c - 2)
                nc.scalar.activation(w_hi[c % 2][:, :, :], raw[:, :, :], ACT.Copy).then_inc(w_hi_ok, 1)

            weight_hi(At(0, 0), 0)
            with act.Fori(0, IMAGES) as image:
                for layer in range(LAYERS):
                    at = At(image, layer)
                    for i in range(CT):
                        act.wait_ge(normed, at.phases(CT, i + 1))
                        act.wait_ge(o_mm, at.phases(2 * CT, 0) + start(o_mm))
                        nc.scalar.activation(a_hi[:, i, :], qk[:, i, :], ACT.Copy).then_inc(a_hi_ok, 1)
                    weight_hi(at, 1)
                    with act.Fori(0, QK_CHUNKS // 2) as i:
                        for s in range(2):
                            act.wait_ge(raw_in, i * 32 + at.phases(16 * CHUNKS, 16 * (s + 3)))
                            act.wait_ge(qk_mm, i * 8 + at.phases(4 * QK_CHUNKS, 4 * (s + 1)))
                            nc.scalar.activation(w_hi[s][:, :, :], raw[:, :, :],
                                                 ACT.Copy).then_inc(w_hi_ok, 1)
                    def prepare(h, step):
                        rows, where = head_rows(h.slot), pos_rows(h.slot)
                        if step == 0:
                            nc.scalar.activation(q_hi[h.slot][rows, :], qk[rows, h.pair, :],
                                                 ACT.Copy).then_inc(q_hi_ok, 1)
                        elif step == 4 and layer == 0:
                            nc.scalar.activation(q_rel[rows, :], qk[rows, h.pair, :],
                                                 ACT.Copy).then_inc(q_rel_ok, 1)
                        elif step == 5:
                            nc.scalar.activation(v_head[h.slot][:, :, :],
                                                 v[:, :, bass.ds(h.pair * 128 + h.slot * 64, HEAD_DIM)],
                                                 ACT.Copy).then_inc(v_head_ok, 1)
                        elif step == 1:
                            nc.scalar.activation(k_hi[h.slot][rows, :], qk[rows, h.pair + CT, :],
                                                 ACT.Copy).then_inc(k_hi_ok, 1)
                        elif step == 2:
                            nc.scalar.activation(q_max[h.slot][rows, :], qk[rows, h.pair, :],
                                                 ACT.Copy).then_inc(q_max_ok, 1)
                        elif step == 3 and layer == 0:
                            act.wait_ge(pos_mm, h.heads0(1, 1))
                            a = where.start
                            nc.scalar.activation(q_hi[h.slot][a:a + SIDE, :], small_all[a:a + SIDE, :],
                                                 ACT.Copy).then_inc(pos_hi_ok, 1)
                            nc.scalar.activation(
                                q_hi[h.slot][a + SIDE:a + 2 * SIDE, :].rearrange("p (h w) -> p w h", w=SIDE),
                                small_all[a + SIDE:a + 2 * SIDE, :].rearrange("p (w h) -> p w h", h=SIDE),
                                ACT.Copy).then_inc(pos_hi_ok, 1)

                    def sums_copy(h):
                        act.wait_ge(sum_mm, h.heads(1, 1) + start(sum_mm))
                        act.wait_ge(recip_ok, h.heads(1, 0) + start(recip_ok))
                        nc.scalar.activation(sums[:, :], small[:, 0, :], ACT.Copy).then_inc(sums_out, 1)

                    def main(h, nxt, first):
                        if nxt is not None:
                            prepare(nxt, 0)
                            prepare(nxt, 4 if layer == 0 else 1)
                        r = max_row(h.slot)
                        act.wait_ge(max_row_mm, h.heads(1, 1))
                        nc.scalar.activation(q_max[h.slot][r:r + 1, HALF:], small[r:r + 1, 1, :],
                                             ACT.Copy).then_inc(max_row2_ok, 1)
                        for t in range(QT):
                            if nxt is not None and t == 2:
                                prepare(nxt, 3)
                            a, b = query_span(layer, ORDER[layer][t])
                            act.wait_ge(score_ok, h.heads(QT, t + 1))
                            act.wait_ge(pv_done, h.heads(QT, t + 1 - P_SLOTS) + start(pv_done))
                            act.wait_ge(added, h.heads(QT, t + 1 - P_SLOTS) + start(added))
                            nc.scalar.activation(
                                prob[:, t % P_SLOTS, 0:b - a],
                                score[:, t % 2, :, :].rearrange("p a b -> p (a b)")[:, 0:b - a],
                                ACT.Exp).then_inc(prob_ok, 1)
                            if not first and t == 0:
                                sums_copy(At(image, layer, h.pair if h.slot else h.pair - 1, 1 - h.slot))
                            if nxt is not None and t == 0 and layer == 0:
                                prepare(nxt, 1)
                            if nxt is not None and t == 3:
                                act.wait_ge(pv_done, h.heads(QT, 0) + start(pv_done))
                                prepare(nxt, 5)
                                prepare(nxt, 2)

                    head = At(image, layer, 0, 0)
                    for c in range(V_CHUNKS):
                        for t in range(QT):
                            n = c * QT + t
                            if c == V_CHUNKS - 1 and t == 0:
                                act.wait_ge(v_mm, at.phases(V_CHUNKS * QT, c * QT))
                                prepare(head, 0)
                                prepare(head, 1)
                            if c == V_CHUNKS - 1 and t == 2:
                                prepare(head, 3)
                            act.wait_ge(v_mm, at.phases(V_CHUNKS * QT, n + 1))
                            nc.scalar.activation(v[:, t, c * CHUNK:(c + 1) * CHUNK],
                                                 score[:, n // 2 % 2, n % 2, 0:CHUNK],
                                                 ACT.Copy).then_inc(v_ok, 1)
                        if c == 0:
                            weight_hi(at, QK_CHUNKS + 2)

                    def prepare_all(h):
                        prepare(h, 2)
                        act.wait_ge(v_ok, at.phases(V_CHUNKS * QT, V_CHUNKS * QT))
                        prepare(h, 5)

                    each_head(act, image, layer, prepare_all, main)
                    weight_hi(at, QK_CHUNKS + V_CHUNKS)
                    sums_copy(At(image, layer, HEADS // 2 - 1, 1))
                    for i in range(CT):
                        act.wait_ge(sum_mm, at.phases(HEADS, HEADS) + start(sum_mm))
                        act.wait_ge(head_done, at.phases(HEADS, HEADS if i == CT - 1 else HEADS - 2)
                                    + start(head_done))
                        if layer == 0:
                            nc.scalar.activation(a_hi[:, i, :], qk[:, i, :], ACT.Identity,
                                                 bias=bv[:, i:i + 1]).then_inc(o_hi_ok, 1)
                        else:
                            nc.scalar.activation(a_hi[:, i, :], qk[:, i, :], ACT.Copy).then_inc(o_hi_ok, 1)
                    weight_hi(at, QK_CHUNKS + V_CHUNKS + 1)
                    weight_hi(at, CHUNKS - 1)
                    weight_hi(at.after(), 0)

        @block.vector
        def _(dve):
            def weight_lo(at, c, more=0, s=None):
                dve.wait_ge(w_hi_ok, more + at.phases(CHUNKS, c + 1) + start(w_hi_ok))
                s = c % 2
                nc.vector.tensor_tensor(w_lo[s][:, :, :], raw[:, :, :], w_hi[s][:, :, :].bitcast(F32),
                                        ALU.subtract).then_inc(w_lo_ok, 1)

            nc.vector.memset(ones[:, :], 1.0).then_inc(const_ok, 1)
            nc.vector.memset(power[:, :], -0.5).then_inc(const_ok, 1)
            for s in range(2):
                nc.vector.memset(k_lo[s][pos_rows(s), :].bitcast(F32), 0.0).then_inc(const_ok, 1)
                nc.vector.memset(q_max[s][pos_rows(s), :].bitcast(F32), 0.0).then_inc(const_ok, 1)
            dve.wait_ge(const_ok, 6)
            for s in range(2):
                r = max_row(s)
                nc.vector.memset(k_lo[s][r:r + 1, :].bitcast(F32), -1.0).then_inc(const_ok, 1)
            dve.wait_ge(const_in, 16 * 8)
            nc.vector.tensor_copy(ident[:, :], qk[:, 0, 0:128]).then_inc(const_ok, 1)
            for s in range(2):
                nc.vector.tensor_copy(k_hi[s][pos_rows(s), :], qk[pos_rows(s), 1, :]).then_inc(const_ok, 1)
            dve.wait_ge(const_ok, N_SETUP)

            def statistics(at, i):
                src = qk[:, CT + i, :] if at.layer == 0 else x[:, i, :]
                for half in range(2):
                    nc.vector.bn_stats(bn[:, i, half, :], src[:, half * HALF:(half + 1) * HALF])\
                        .then_inc(bn_ok, 1)

            def aggregate(at):
                wait_apart(dve, bn_ok, at.phases(2 * CT, 2 * CT))
                for i in range(CT):
                    nc.vector.bn_aggr(mean_var[:, i, :], bn[:, i, :, :].rearrange("p a b -> p (a b)"))\
                        .then_inc(mv_ok, 1)

            def group_means(at):
                dve.wait_ge(gsum_ok, at.phases(1, 1))
                nc.vector.tensor_copy(group_mv[:, :, :],
                                      small[:, 0, 0:2 * CT].rearrange("p (i k) -> p i k", k=2))\
                    .then_inc(gmv_ok, 1)
                dve.wait_ge(gmv_ok, at.phases(1, 1))
                dve.wait_ge(mv_ok, at.phases(CT, CT))
                nc.vector.tensor_tensor(shift2[:, 0, :], mean_var[:, :, 0], group_mv[:, :, 0],
                                        ALU.subtract).then_inc(shift_ok, 1)
                dve.wait_ge(shift_ok, at.phases(1, 1))
                nc.vector.tensor_tensor(shift2[:, 1, :], shift2[:, 0, :], shift2[:, 0, :],
                                        ALU.mult).then_inc(shift2_ok, 1)

            def group_variances(at):
                dve.wait_ge(gshift_ok, at.phases(1, 1))
                nc.vector.scalar_tensor_tensor(variance[:, :], small[:, 1, 0:CT], EPS,
                                               group_mv[:, :, 1], ALU.add, ALU.add).then_inc(var_ok, 1)

            def norm(at, i):
                dve.wait_ge(rstd_ok, at.phases(1, 1))
                src = qk[:, CT + i, :] if at.layer == 0 else x[:, i, :]
                nc.vector.tensor_scalar(qk[:, i, :], src, group_mv[:, i, 0:1],
                                        rstd[:, i:i + 1], ALU.subtract, ALU.mult).then_inc(normed, 1)

            dve.wait_ge(next_in, 16)
            for i in range(CT):
                statistics(At(0, 0), i)
            aggregate(At(0, 0))
            group_means(At(0, 0))
            group_variances(At(0, 0))
            weight_lo(At(0, 0), 0)
            for i in range(CT):
                norm(At(0, 0), i)
            with dve.Fori(0, IMAGES) as image:
                for layer in range(LAYERS):
                    at = At(image, layer)
                    if layer == 1:
                        norm(at, 0)
                    for i in range(CT):
                        if layer == 1 and i + 1 < CT:
                            norm(at, i + 1)
                        dve.wait_ge(a_hi_ok, at.phases(CT, i + 1))
                        nc.vector.tensor_tensor(a_lo[:, i, :], qk[:, i, :], a_hi[:, i, :].bitcast(F32),
                                                ALU.subtract).then_inc(a_lo_ok, 1)
                    weight_lo(at, 1)
                    with dve.Fori(0, QK_CHUNKS // 2) as i:
                        for s in range(2):
                            for k in range(4):
                                n, o = 4 * s + k, 2 * s + k // 2
                                dve.wait_ge(qk_mm, i * 8 + at.phases(4 * QK_CHUNKS, n + 1))
                                tile = i * 4 + o
                                dst = qk[:, tile, (k % 2) * HALF:(k % 2 + 1) * HALF]
                                src = score[:, n // 2 % 2, n % 2, :]
                                if layer == 0:
                                    nc.vector.tensor_scalar(dst, src, bqk[:, bass.ds(tile, 1)],
                                                            scale[:, bass.ds(tile, 1)],
                                                            ALU.add, ALU.mult).then_inc(qk_ok, 1)
                                else:
                                    nc.vector.tensor_scalar(dst, src, scale[:, bass.ds(tile, 1)], None,
                                                            ALU.mult).then_inc(qk_ok, 1)
                            weight_lo(at, s + 2, i * 2)
                    weight_lo(at, QK_CHUNKS + 2)
                    if layer == 1:
                        wait_apart(dve, stage_in, image * 16 + 16)
                        dve.wait_ge(v_mm, at.phases(V_CHUNKS * QT, (V_CHUNKS - 1) * QT))
                        for s in range(2):
                            nc.vector.tensor_copy(q_hi[s][pos_rows(s), :], stage[pos_rows(s), :])\
                                .then_inc(mask_ok, 1)
                        wait_apart(dve, mask_ok, image * 4 + 2)
                        for s in range(2):
                            nc.vector.memset(q_lo[s][pos_rows(s), :].bitcast(F32), 0.0)\
                                .then_inc(mask_ok, 1)

                    def prepare(h, part):
                        rows, where, s = head_rows(h.slot), pos_rows(h.slot), h.slot
                        if part == 0:
                            dve.wait_ge(q_hi_ok, h.heads(1, 1))
                            nc.vector.tensor_tensor(q_lo[s][rows, :], qk[rows, h.pair, :],
                                                    q_hi[s][rows, :].bitcast(F32),
                                                    ALU.subtract).then_inc(q_lo_ok, 1)
                        if part == 1:
                            dve.wait_ge(k_hi_ok, h.heads(1, 1))
                            nc.vector.tensor_tensor(k_lo[s][rows, :], qk[rows, h.pair + CT, :],
                                                    k_hi[s][rows, :].bitcast(F32),
                                                    ALU.subtract).then_inc(k_lo_ok, 1)
                        if part == 2 and layer == 0:
                            a = where.start
                            dve.wait_ge(pos_hi_ok, h.heads0(2, 1))
                            nc.vector.tensor_tensor(q_lo[s][a:a + SIDE, :], small_all[a:a + SIDE, :],
                                                    q_hi[s][a:a + SIDE, :].bitcast(F32),
                                                    ALU.subtract).then_inc(pos_lo_ok, 1)
                            dve.wait_ge(pos_hi_ok, h.heads0(2, 2))
                            a += SIDE
                            nc.vector.tensor_tensor(
                                q_lo[s][a:a + SIDE, :].rearrange("p (h w) -> p w h", w=SIDE),
                                small_all[a:a + SIDE, :].rearrange("p (w h) -> p w h", h=SIDE),
                                q_hi[s][a:a + SIDE, :].rearrange("p (h w) -> p w h", w=SIDE).bitcast(F32),
                                ALU.subtract).then_inc(pos_lo_ok, 1)

                    def maxima(h, first=False):
                        for n in range(MAX_PER[layer]):
                            t = n // 2 if layer == 0 else n
                            size = HALF if layer == 0 else key_span(t)[1] - key_span(t)[0]
                            dve.wait_ge(max_mm, h.heads2(*MAX_PER, n + 1))
                            nc.vector.reduce_max(max_part[:, n:n + 1], small[:, n % 2, 0:size],
                                                 AX.X).then_inc(max_part_ok, 1)
                        dve.wait_ge(max_part_ok, h.heads2(*MAX_PER, MAX_PER[layer]))
                        if first:
                            wait_apart(dve, cols_zero, at.phases(1, 1))
                        dst = max_cols[:, 64:].rearrange("p (t c) -> p t c", c=128)[:, :, 0]
                        if layer == 0:
                            both = max_part[:, :].rearrange("p (t k) -> p t k", k=2)
                            nc.vector.tensor_tensor(dst, both[:, :, 0], both[:, :, 1],
                                                    ALU.max).then_inc(max_cols_ok, 1)
                        else:
                            nc.vector.tensor_copy(dst, max_part[:, 0:QT]).then_inc(max_cols_ok, 1)

                    def invert(h):
                        dve.wait_ge(sums_out, h.heads(1, 1))
                        dve.wait_ge(head_done, h.heads(1, 0) + start(head_done))
                        nc.vector.reciprocal(recip[:, :], sums[:, :]).then_inc(recip_ok, 1)

                    def normalise(h):
                        dve.wait_ge(recip_ok, h.heads(1, 1) + start(recip_ok))
                        rows = head_rows(h.slot)
                        for half in range(2):
                            part = head_rows(half)
                            last = nc.vector.tensor_tensor(
                                qk[rows, h.pair, half * HALF:(half + 1) * HALF],
                                head_out[part, h.slot, :], recip[part, :], ALU.mult)
                            last.then_inc(*((head_done, 1) if half else (recip_used, 1)))

                    def prepare_all(h):
                        prepare(h, 0)
                        prepare(h, 1)
                        prepare(h, 2)
                        maxima(h, True)

                    def main(h, nxt, first):
                        r = max_row(h.slot)
                        before = At(image, layer, h.pair if h.slot else h.pair - 1, 1 - h.slot)
                        dve.wait_ge(max_row_mm, h.heads(1, 1))
                        nc.vector.tensor_copy(q_max[h.slot][r:r + 1, 0:HALF], small[r:r + 1, 0, :])\
                            .then_inc(max_row_ok, 1)
                        if nxt is not None:
                            prepare(nxt, 0)
                            if layer == 1:
                                prepare(nxt, 1)
                        if not first:
                            invert(before)
                        if nxt is not None and layer == 0:
                            prepare(nxt, 1)
                            prepare(nxt, 2)
                        if not first:
                            normalise(before)
                        if nxt is not None:
                            maxima(nxt)

                    each_head(dve, image, layer, prepare_all, main)
                    weight_lo(at, QK_CHUNKS + V_CHUNKS)
                    last_head = At(image, layer, HEADS // 2 - 1, 1)
                    for i in range(CT):
                        if i == CT // 2:
                            invert(last_head)
                        if i == CT - 1:
                            normalise(last_head)
                        dve.wait_ge(o_hi_ok, at.phases(CT, i + 1))
                        if layer == 0:
                            nc.vector.scalar_tensor_tensor(a_lo[:, i, :], qk[:, i, :], bv[:, i:i + 1],
                                                           a_hi[:, i, :].bitcast(F32), ALU.add,
                                                           ALU.subtract).then_inc(o_lo_ok, 1)
                        else:
                            nc.vector.tensor_tensor(a_lo[:, i, :], qk[:, i, :], a_hi[:, i, :].bitcast(F32),
                                                    ALU.subtract).then_inc(o_lo_ok, 1)
                    weight_lo(at, QK_CHUNKS + V_CHUNKS + 1)
                    nx = at.after()
                    if layer == 0:
                        wait_apart(dve, x_in_sem, image * 16 + 16)
                    for n in range(2 * CT):
                        o, half = n // 2, n % 2
                        dve.wait_ge(o_mm, at.phases(2 * CT, n + 1) + start(o_mm))
                        dst = x[:, o, half * HALF:(half + 1) * HALF]
                        src = score[:, n // 2 % 2, n % 2, :]
                        if layer == 0:
                            nc.vector.scalar_tensor_tensor(dst, src, bp[:, o:o + 1], dst, ALU.add,
                                                           ALU.add).then_inc(o_ok, 1)
                        else:
                            nc.vector.tensor_tensor(dst, src, dst, ALU.add).then_inc(o_ok, 1)
                        if n == 3:
                            weight_lo(at, CHUNKS - 1)
                        if layer == 0 and half == 1:
                            dve.wait_ge(o_ok, at.phases(2 * CT, n + 1))
                            statistics(nx, o)
                        if layer == 1:
                            if n == 1:
                                wait_apart(dve, next_in, image * 16 + 32)
                            if n in (1, 2, 3):
                                statistics(nx, 2 * n - 2)
                                statistics(nx, 2 * n - 1)
                            if n == 3:
                                aggregate(nx)
                            if n == NORM_AT:
                                group_means(nx)
                                group_variances(nx)
                            if n > NORM_AT:
                                norm(nx, n - NORM_AT - 1)
                        if n == 2 * CT - 2:
                            weight_lo(nx, 0)
                    if layer == 0:
                        aggregate(nx)
                        group_means(nx)
                        group_variances(nx)

        @block.tensor
        def _(pe):
            def split_product(out, w, a, first, last):
                nc.tensor.matmul(out, w[0], a[0], start=first, stop=False)
                nc.tensor.matmul(out, w[0], a[1], start=False, stop=False)
                return nc.tensor.matmul(out, w[1], a[0], start=False, stop=last)

            pe.wait_ge(const_ok, N_SETUP)

            def averages(bank, stats, width, done):
                spans = CT // GROUP_SPAN
                out = small[:, bank, 0:CT * width].rearrange("p (a j k) -> p a j k", a=spans, k=width)
                for j in range(GROUP_SPAN):
                    from_tiles = [(n, i) for n, (i, k) in enumerate(blocks) if k == j]
                    for k, (n, i) in enumerate(from_tiles):
                        last = nc.tensor.matmul(out[:, :, j, :], group[:, n, :], stats(i),
                                                start=(k == 0), stop=(k == len(from_tiles) - 1))
                last.then_inc(done, 1)

            def group_averages(at):
                pe.wait_ge(mv_ok, at.phases(CT, CT))
                averages(0, lambda i: mean_var[:, :, :].rearrange(
                    "p (a i) k -> p a i k", i=GROUP_SPAN)[:, :, i, :], 2, gsum_ok)
                pe.wait_ge(shift2_ok, at.phases(1, 1))
                averages(1, lambda i: shift2[:, 1, :].rearrange(
                    "p (a i) -> p a i", i=GROUP_SPAN)[:, :, i:i + 1], 1, gshift_ok)

            group_averages(At(0, 0))
            with pe.Fori(0, IMAGES) as image:
                for layer in range(LAYERS):
                    at = At(image, layer)
                    with pe.Fori(0, QK_CHUNKS // 2) as i:
                        for s in range(2):
                            pe.wait_ge(w_hi_ok, i * 2 + at.phases(CHUNKS, s + 1) + start(w_hi_ok))
                            pe.wait_ge(w_lo_ok, i * 2 + at.phases(CHUNKS, s + 1) + start(w_lo_ok))
                            for k in range(0, 4, 2):
                                n, cols = 4 * s + k, slice(k * 64, k * 64 + 128)
                                pe.wait_ge(qk_ok, i * 8 + at.phases(4 * QK_CHUNKS, n - 2) + start(qk_ok))
                                for c in range(CT):
                                    if s == 0 and k == 0:
                                        pe.wait_ge(a_lo_ok, at.phases(CT, c + 1))
                                    for half in range(2):
                                        tokens = slice(half * HALF, (half + 1) * HALF)
                                        last = split_product(score[:, n // 2 % 2, half, :],
                                                             (w_hi[s][:, c, cols], w_lo[s][:, c, cols]),
                                                             (a_hi[:, c, tokens], a_lo[:, c, tokens]),
                                                             c == 0, c == CT - 1)
                                        if c == CT - 1:
                                            last.then_inc(qk_mm, 1)
                    def position(h, first=False):
                        rows, a = head_rows(h.slot), pos_rows(h.slot).start
                        if first:
                            wait_apart(pe, qk_ok, at.phases(4 * QK_CHUNKS, 4 * QK_CHUNKS) + start(qk_ok))
                            q = qk[rows, 0, :]
                        else:
                            wait_apart(pe, q_rel_ok, h.image * (HEADS - 1) + h.pair * 2 + h.slot)
                            q = q_rel[rows, :]
                        by_row = q.rearrange("p (h w) -> p h w", w=SIDE)
                        for i in range(SIDE):
                            window = slice(SIDE - 1 - i, 2 * SIDE - 1 - i)
                            nc.tensor.matmul(small_all[a:a + SIDE, i * SIDE:(i + 1) * SIDE],
                                             rel[rows, 0, window], by_row[:, i, :], start=True, stop=True)
                            last = nc.tensor.matmul(small_all[a + SIDE:a + 2 * SIDE, i * SIDE:(i + 1) * SIDE],
                                                    rel[rows, 1, window], by_row[:, :, i],
                                                    start=True, stop=True)
                        last.then_inc(pos_mm, 1)

                    def maximum(h, n):
                        s, t = h.slot, (n // 2 if layer == 0 else n)
                        a, b = (n % 2 * HALF, (n % 2 + 1) * HALF) if layer == 0 else key_span(t)
                        if n == 0:
                            pe.wait_ge(q_hi_ok, h.heads(1, 1))
                            pe.wait_ge(k_hi_ok, h.heads(1, 1))
                            if layer == 0:
                                pe.wait_ge(pos_lo_ok, h.heads0(2, 2))
                            else:
                                pe.wait_ge(mask_ok, image * 4 + 4)
                        if n >= 2:
                            pe.wait_ge(max_part_ok, h.heads2(*MAX_PER, n - 1))
                        nc.tensor.matmul(small[:, n % 2, 0:b - a], q_hi[s][:, t * 128:(t + 1) * 128],
                                         k_hi[s][:, a:b], start=True, stop=True).then_inc(max_mm, 1)

                    def maximum_row(h):
                        pe.wait_ge(max_cols_ok, h.heads(1, 1))
                        for t in range(QT):
                            a = t * 128 + 64 * h.slot
                            last = nc.tensor.matmul(small_all[:, t * 128:(t + 1) * 128],
                                                    max_cols[:, a:a + 128], ident[:, :],
                                                    start=True, stop=True)
                        last.then_inc(max_row_mm, 1)

                    def scores(h, step, part):
                        s, t = h.slot, ORDER[layer][step]
                        a, b = query_span(layer, t)
                        keys = slice(t * 128, (t + 1) * 128)
                        pieces = [(a, a + HALF), (a + HALF, b)] if b - a > HALF else [(a, b)]
                        if part == 0:
                            pe.wait_ge(prob_ok, h.heads(QT, step - 1) + start(prob_ok))
                            if step == 0:
                                pe.wait_ge(q_lo_ok, h.heads(1, 1))
                        elif step == 0:
                            pe.wait_ge(k_lo_ok, h.heads(1, 1))
                            pe.wait_ge(q_max_ok, h.heads(1, 1))
                            pe.wait_ge(max_row_ok, h.heads(1, 1))
                            pe.wait_ge(max_row2_ok, h.heads(1, 1))
                        for w, x_ in (((k_lo, q_max),) if part else ((k_hi, q_hi), (k_hi, q_lo))):
                            for n, (p, q) in enumerate(pieces):
                                last = nc.tensor.matmul(score[:, step % 2, n, 0:q - p], w[s][:, keys],
                                                        x_[s][:, p:q], start=(x_ is q_hi), stop=(part == 1))
                        if part == 1:
                            last.then_inc(score_ok, 1)

                    def values(h, step):
                        s = h.slot
                        steps = [step] if layer == 0 else [step - 1, step]
                        if step == 0 or (layer == 1 and step == 1):
                            pe.wait_ge(v_head_ok, h.heads(1, 1))
                            pe.wait_ge(head_done, h.heads(1, -1) + start(head_done))
                        pe.wait_ge(prob_ok, h.heads(QT, step + 1) + start(prob_ok))
                        for u in steps:
                            t = ORDER[layer][u]
                            a, b = query_span(layer, t)
                            for half in range(2):
                                p, q = max(a, half * HALF), min(b, (half + 1) * HALF)
                                if p >= q:
                                    continue
                                first = (u == 0 or (layer == 1 and u == 1))
                                last_u = QT - 1 if layer == 0 else QT - 1
                                out = head_out[head_rows(half), s, p - half * HALF:q - half * HALF]
                                last = nc.tensor.matmul(out, v_head[s][:, t, :],
                                                        prob[:, u % P_SLOTS, p - a:q - a],
                                                        start=first, stop=(u == last_u),
                                                        skip_group_check=(layer == 1))
                        last.then_inc(pv_done, len(steps))

                    def sums(h):
                        pe.wait_ge(added, h.heads(QT, QT) + start(added))
                        for half in range(2):
                            last = nc.tensor.matmul(small[head_rows(half), 0, :], ones[:, :],
                                                    acc[h.slot][:, half * HALF:(half + 1) * HALF],
                                                    start=True, stop=True)
                        last.then_inc(sum_mm, 1)

                    head, made = At(image, layer, 0, 0), 0
                    for c in range(V_CHUNKS):
                        chunk, s = QK_CHUNKS + c, c % 2
                        pe.wait_ge(w_lo_ok, at.phases(CHUNKS, chunk + 1) + start(w_lo_ok))
                        for t in range(QT):
                            if c == V_CHUNKS - 1 and t == 1 and layer == 0:
                                position(head, True)
                            n = c * QT + t
                            if n < 4:
                                pe.wait_ge(qk_ok, at.phases(4 * QK_CHUNKS, 4 * QK_CHUNKS - 3 + n) + start(qk_ok))
                            else:
                                pe.wait_ge(v_ok, at.phases(V_CHUNKS * QT, n - 3))
                            tok = slice(t * 128, (t + 1) * 128)
                            for i in range(CT):
                                last = split_product(score[:, n // 2 % 2, n % 2, 0:CHUNK],
                                                     (a_hi[:, i, tok], a_lo[:, i, tok]),
                                                     (w_hi[s][:, i, :], w_lo[s][:, i, :]),
                                                     i == 0, i == CT - 1)
                                if c == V_CHUNKS - 1 and t >= 3 and i % MAX_EVERY[layer] == \
                                        MAX_EVERY[layer] - 1 and made < MAX_PER[layer]:
                                    maximum(head, made)
                                    made += 1
                            last.then_inc(v_mm, 1)

                    for n in range(made, MAX_PER[layer]):
                        maximum(head, n)

                    def prepare(h):
                        pe.wait_ge(v_ok, at.phases(V_CHUNKS * QT, V_CHUNKS * QT))

                    def main(h, nxt, first):
                        before = None
                        if not first:
                            before = At(image, layer, h.pair if h.slot else h.pair - 1, 1 - h.slot)

                        def maxima(t, part):
                            if nxt is not None:
                                for n in max_turn(layer, t, part):
                                    maximum(nxt, n)

                        for t in range(QT):
                            scores(h, t, 0)
                            if t == 0:
                                maximum_row(h)
                                if before is not None:
                                    values(before, QT - 1)
                            maxima(t, 0)
                            scores(h, t, 1)
                            maxima(t, 1)
                            if t > 0 and (layer == 0 or t % 2 == 0):
                                values(h, t - 1)
                            maxima(t, 2)
                            if t == 0 and before is not None:
                                sums(before)
                            if t == 1:
                                if before is not None:
                                    pe.wait_ge(sums_out, before.heads(1, 1))
                                if nxt is not None and layer == 0:
                                    position(nxt)
                        if nxt is None:
                            values(h, QT - 1)
                            sums(h)

                    each_head(pe, image, layer, prepare, main)
                    def output(n, c, chunk):
                        o, half, s = n // 2, n % 2, chunk % 2
                        cols, h = slice(o % 2 * 128, o % 2 * 128 + 128), slice(half * HALF, (half + 1) * HALF)
                        last = split_product(score[:, n // 2 % 2, n % 2, :],
                                             (w_hi[s][:, c, cols], w_lo[s][:, c, cols]),
                                             (a_hi[:, c, h], a_lo[:, c, h]), c == 0, c == CT - 1)
                        if c == CT - 1:
                            last.then_inc(o_mm, 1)

                    chunk = QK_CHUNKS + V_CHUNKS
                    pe.wait_ge(w_lo_ok, at.phases(CHUNKS, chunk + 1) + start(w_lo_ok))
                    for c in range(CT):
                        pe.wait_ge(o_lo_ok, at.phases(CT, c + 1))
                        for n in range(4):
                            output(n, c, chunk)
                    for n in range(4, 2 * CT):
                        chunk = QK_CHUNKS + V_CHUNKS + n // 4
                        if n % 4 == 0:
                            pe.wait_ge(w_lo_ok, at.phases(CHUNKS, chunk + 1) + start(w_lo_ok))
                        pe.wait_ge(o_ok, at.phases(2 * CT, n - 3))
                        for c in range(CT):
                            output(n, c, chunk)
                        if layer == 1 and n == NORM_AT:
                            group_averages(at.after())
                    if layer == 0:
                        group_averages(at.after())


def kernel(**inputs):
    import numpy as np
    import concourse.bacc as bacc
    from concourse.bass_utils import run_bass_kernel_spmd

    f32 = np.float32

    def tiles(a):
        a = np.asarray(a)
        return np.ascontiguousarray(a.reshape(CT, 128, -1).transpose(1, 0, 2))

    def vector_tiles(a):
        return np.ascontiguousarray(np.asarray(a).reshape(-1, 128).T)

    def chunks(w):
        w = tiles(w)
        return [w[:, :, n:n + CHUNK].reshape(128, CT * CHUNK) for n in range(0, w.shape[2], CHUNK)]

    x = np.asarray(inputs["x"])
    x_t = x.reshape(IMAGES, TOKENS, CT, 128).transpose(0, 3, 2, 1)
    qkv = np.asarray(inputs["L1_conv_qkv_w"])
    weights = np.stack([
        np.stack(sum((chunks(inputs[f"L0_conv_W{n}"]) for n in "qkvp"), [])),
        np.stack(chunks(qkv.T) + chunks(np.asarray(inputs["L1_conv_out_w"]).T)),
    ])
    rel = np.stack([np.asarray(inputs[f"L0_conv_rel_{n}"])[::-1].T for n in "hw"], axis=1)
    token = np.arange(TOKENS)
    line = np.arange(SIDE)
    onehot = np.concatenate([token // SIDE == line[:, None], token % SIDE == line[:, None]]).astype(f32)
    near = np.clip(line, RADIUS, SIDE - 1 - RADIUS)
    far = np.abs(near[None, :] - line[:, None]) > RADIUS
    mask = np.where(np.concatenate([far[:, token // SIDE], far[:, token % SIDE]]), f32(-2.0 ** 100), f32(0))
    channel = np.arange(GROUP_SPAN * 128)
    same = (channel[:, None] // GROUP == channel[None, :] // GROUP) * (1.0 / GROUP)
    group = np.stack([same[i * 128:(i + 1) * 128, j * 128:(j + 1) * 128] for i, j in group_blocks()], axis=1)
    scale = np.ones((128, QK_TILES), f32)
    scale[:, CT:] = HEAD_DIM ** -0.5
    arrays = {
        "x_t": np.concatenate([x_t, x_t[:1]]),
        "weights": weights,
        "bias_qk": np.concatenate([vector_tiles(inputs[f"L0_conv_b{n}"]) for n in "qk"], axis=1),
        "scale_qk": scale,
        "bias_v": vector_tiles(inputs["L0_conv_bv"]),
        "bias_out": vector_tiles(inputs["L0_conv_bp"]),
        "rel": np.concatenate([rel, rel]),
        "onehot": np.concatenate([onehot, onehot]),
        "mask": np.concatenate([mask, mask]).astype(f32),
        "group": group.astype(f32),
        "ident": np.eye(128, dtype=f32),
    }
    arrays = {k: np.ascontiguousarray(a) for k, a in arrays.items()}
    nc = bacc.Bacc("TRN2", target_bir_lowering=False, num_devices=1)
    args = [nc.dram_tensor(k, a.shape, mybir.dt.from_np(a.dtype), kind="ExternalInput").ap()
            for k, a in arrays.items()]
    y = nc.dram_tensor("y_t", (IMAGES, 128, CT, TOKENS), F32, kind="ExternalOutput").ap()
    build(nc, *args, y)
    r = run_bass_kernel_spmd(nc, [arrays], core_ids=[0])
    y_t = np.asarray(r.results[0]["y_t"])
    return np.ascontiguousarray(y_t.transpose(0, 3, 2, 1)).reshape(x.shape)
```
